# Optimizing a Trainium2 kernel written in Bass

```python
import numpy as np
import jax
import jax.numpy as jnp

def _softmax(x, axis=-1):
    return jax.nn.softmax(x, axis=axis)

def _gelu(x):
    return jax.nn.gelu(x, approximate=True)

def _silu(x):
    return jax.nn.silu(x)

def _sigmoid(x):
    return jax.nn.sigmoid(x)

def _layernorm(x, axis=-1, eps=1e-05):
    m = jnp.mean(x, axis=axis, keepdims=True)
    v = jnp.var(x, axis=axis, keepdims=True)
    return (x - m) / jnp.sqrt(v + eps)

def _scatter_add(tgt, idx, src, axis=0):
    return tgt.at[idx].add(src)

def _segment_sum(src, seg, n):
    return jax.ops.segment_sum(src, seg, n)
kernel_name = 'mk_seq_preln_d1_jaxref_r8_fe5d90'

def setup_inputs(seed: int=0):
    np.random.seed(seed)
    _w = jnp.asarray

    def _L0_attn_setup():
        import jax, jax.numpy as jnp
        import numpy as np
        D_MODEL, D_INNER, D_STATE = (128, 256, 16)
        BATCH, SEQ = (4, 256)

        def silu(x):
            return x * jax.nn.sigmoid(x)

        def selective_scan(u, delta, A, B, C, D):
            bsz = u.shape[0]

            def step(h, xs):
                u_t, dt_t, B_t, C_t = xs
                dA = jnp.exp(dt_t[..., None] * A)
                dBu = (dt_t * u_t)[..., None] * B_t[:, None, :]
                h = h * dA + dBu
                y_t = jnp.einsum('bds,bs->bd', h, C_t) + D * u_t
                return (h, y_t)
            h0 = jnp.zeros((bsz, u.shape[2], A.shape[1]), u.dtype)
            xs = (u.swapaxes(0, 1), delta.swapaxes(0, 1), B.swapaxes(0, 1), C.swapaxes(0, 1))
            _, ys = jax.lax.scan(step, h0, xs)
            return ys.swapaxes(0, 1)
        key = jax.random.key(seed)
        ks = jax.random.split(key, 11)
        s_in = 1.0 / np.sqrt(D_MODEL)
        s_inner = 1.0 / np.sqrt(D_INNER)
        return {'x': jax.random.normal(ks[0], (BATCH, SEQ, D_MODEL), jnp.float32), 'W_in': jax.random.normal(ks[1], (D_MODEL, 2 * D_INNER), jnp.float32) * s_in, 'b_in': jax.random.normal(ks[2], (2 * D_INNER,), jnp.float32) * s_in, 'W_xproj': jax.random.normal(ks[3], (D_INNER, 2 * D_STATE), jnp.float32) * s_inner, 'b_xproj': jax.random.normal(ks[4], (2 * D_STATE,), jnp.float32) * s_inner, 'W_dt': jax.random.normal(ks[5], (D_INNER, D_INNER), jnp.float32) * s_inner, 'b_dt': jax.random.normal(ks[6], (D_INNER,), jnp.float32) * s_inner, 'W_out': jax.random.normal(ks[7], (D_INNER, D_MODEL), jnp.float32) * s_inner, 'b_out': jax.random.normal(ks[8], (D_MODEL,), jnp.float32) * s_inner, 'A_log': jax.random.uniform(ks[9], (D_INNER, D_STATE), jnp.float32, 0.0, np.log(16.0)), 'D_param': jnp.ones((D_INNER,), jnp.float32)}
    _L0_attn_in = _L0_attn_setup()

    def _L0_ffn_setup():
        import jax, jax.numpy as jnp
        import numpy as np
        DIM = 128
        INTER = 256
        E = 8
        TOPK = 2
        ROUTE_SCALE = 1.0

        def _mlp(x, w1, w2, w3):
            h = jax.nn.silu(x @ w1.T) * (x @ w3.T)
            return h @ w2.T
        key = jax.random.key(seed)
        ks = jax.random.split(key, 10)
        s_in = 0.02
        return {'x': jax.random.normal(ks[0], (4, 256, DIM), dtype=jnp.float32), 'gate_w': jax.random.normal(ks[1], (E, DIM), dtype=jnp.float32) * s_in, 'gate_bias': jax.random.normal(ks[2], (E,), dtype=jnp.float32) * 0.01, 'w1': jax.random.normal(ks[3], (E, INTER, DIM), dtype=jnp.float32) * s_in, 'w2': jax.random.normal(ks[4], (E, DIM, INTER), dtype=jnp.float32) * s_in, 'w3': jax.random.normal(ks[5], (E, INTER, DIM), dtype=jnp.float32) * s_in, 'sw1': jax.random.normal(ks[6], (INTER, DIM), dtype=jnp.float32) * s_in, 'sw2': jax.random.normal(ks[7], (DIM, INTER), dtype=jnp.float32) * s_in, 'sw3': jax.random.normal(ks[8], (INTER, DIM), dtype=jnp.float32) * s_in}
    _L0_ffn_in = _L0_ffn_setup()
    _d = {'L0_attn_x': _L0_attn_in['x'], 'L0_attn_W_in': _L0_attn_in['W_in'], 'L0_attn_b_in': _L0_attn_in['b_in'], 'L0_attn_W_xproj': _L0_attn_in['W_xproj'], 'L0_attn_b_xproj': _L0_attn_in['b_xproj'], 'L0_attn_W_dt': _L0_attn_in['W_dt'], 'L0_attn_b_dt': _L0_attn_in['b_dt'], 'L0_attn_W_out': _L0_attn_in['W_out'], 'L0_attn_b_out': _L0_attn_in['b_out'], 'L0_attn_A_log': _L0_attn_in['A_log'], 'L0_attn_D_param': _L0_attn_in['D_param'], 'L0_ffn_gate_w': _L0_ffn_in['gate_w'], 'L0_ffn_gate_bias': _L0_ffn_in['gate_bias'], 'L0_ffn_w1': _L0_ffn_in['w1'], 'L0_ffn_w2': _L0_ffn_in['w2'], 'L0_ffn_w3': _L0_ffn_in['w3'], 'L0_ffn_sw1': _L0_ffn_in['sw1'], 'L0_ffn_sw2': _L0_ffn_in['sw2'], 'L0_ffn_sw3': _L0_ffn_in['sw3']}
    _x0 = _d['L0_attn_x']
    _d['L0_attn_x'] = jax.random.normal(jax.random.fold_in(jax.random.key(seed), 1), (16, 512, 128), dtype=_x0.dtype)
    del _x0
    return _d

def reference(L0_attn_x, L0_attn_W_in, L0_attn_b_in, L0_attn_W_xproj, L0_attn_b_xproj, L0_attn_W_dt, L0_attn_b_dt, L0_attn_W_out, L0_attn_b_out, L0_attn_A_log, L0_attn_D_param, L0_ffn_gate_w, L0_ffn_gate_bias, L0_ffn_w1, L0_ffn_w2, L0_ffn_w3, L0_ffn_sw1, L0_ffn_sw2, L0_ffn_sw3):

    def _L0_attn_ref(x, W_in, b_in, W_xproj, b_xproj, W_dt, b_dt, W_out, b_out, A_log, D_param):
        import jax, jax.numpy as jnp
        import numpy as np
        D_MODEL, D_INNER, D_STATE = (128, 256, 16)
        BATCH, SEQ = (4, 256)

        def silu(x):
            return x * jax.nn.sigmoid(x)

        def selective_scan(u, delta, A, B, C, D):
            bsz = u.shape[0]

            def step(h, xs):
                u_t, dt_t, B_t, C_t = xs
                dA = jnp.exp(dt_t[..., None] * A)
                dBu = (dt_t * u_t)[..., None] * B_t[:, None, :]
                h = h * dA + dBu
                y_t = jnp.einsum('bds,bs->bd', h, C_t) + D * u_t
                return (h, y_t)
            h0 = jnp.zeros((bsz, u.shape[2], A.shape[1]), u.dtype)
            xs = (u.swapaxes(0, 1), delta.swapaxes(0, 1), B.swapaxes(0, 1), C.swapaxes(0, 1))
            _, ys = jax.lax.scan(step, h0, xs)
            return ys.swapaxes(0, 1)
        xz = x @ W_in + b_in
        x_proj, z = jnp.split(xz, 2, axis=-1)
        x_conv = silu(x_proj)
        A = -jnp.exp(A_log)
        x_dbl = x_conv @ W_xproj + b_xproj
        B, C = jnp.split(x_dbl, 2, axis=-1)
        dt = jax.nn.softplus(x_conv @ W_dt + b_dt)
        y = selective_scan(x_conv, dt, A, B, C, D_param)
        y = y * silu(z)
        return y @ W_out + b_out

    def _L0_ffn_ref(x, gate_w, gate_bias, w1, w2, w3, sw1, sw2, sw3):
        import jax, jax.numpy as jnp
        import numpy as np
        DIM = 128
        INTER = 256
        E = 8
        TOPK = 2
        ROUTE_SCALE = 1.0

        def _mlp(x, w1, w2, w3):
            h = jax.nn.silu(x @ w1.T) * (x @ w3.T)
            return h @ w2.T
        shape = x.shape
        xt = x.reshape(-1, DIM)
        T = xt.shape[0]
        logits = xt @ gate_w.T
        scores = jax.nn.softmax(logits.astype(jnp.float32), axis=-1)
        original_scores = scores
        biased = scores + gate_bias
        _, indices = jax.lax.top_k(biased, TOPK)
        weights = jnp.take_along_axis(original_scores, indices, axis=1)
        weights = (weights * ROUTE_SCALE).astype(x.dtype)
        combine = (jax.nn.one_hot(indices, E, dtype=weights.dtype) * weights[..., None]).sum(axis=1)
        y = jnp.zeros_like(xt)
        for e in range(E):
            y = y + _mlp(xt, w1[e], w2[e], w3[e]) * combine[:, e:e + 1]
        z = _mlp(xt, sw1, sw2, sw3)
        return (y + z).reshape(shape)
    x = L0_attn_x
    x = x + _L0_attn_ref(_layernorm(x, axis=-1), L0_attn_W_in, L0_attn_b_in, L0_attn_W_xproj, L0_attn_b_xproj, L0_attn_W_dt, L0_attn_b_dt, L0_attn_W_out, L0_attn_b_out, L0_attn_A_log, L0_attn_D_param)
    x = x + _L0_ffn_ref(_layernorm(x, axis=-1), L0_ffn_gate_w, L0_ffn_gate_bias, L0_ffn_w1, L0_ffn_w2, L0_ffn_w3, L0_ffn_sw1, L0_ffn_sw2, L0_ffn_sw3)
    return x

_drawn_inputs = setup_inputs


def setup_inputs(seed=0):
    import zlib

    import numpy as np

    out = dict(_drawn_inputs(seed))
    spreads = {'L0_attn_D_param': (1.0, 0.2)}
    factors = {'L0_attn_b_dt': 3.536,
     'L0_ffn_gate_w': 8.0,
     'L0_ffn_gate_bias': 8.0,
     'L0_ffn_w1': 8.0,
     'L0_ffn_w2': 8.0,
     'L0_ffn_w3': 8.0,
     'L0_ffn_sw1': 8.0,
     'L0_ffn_sw2': 8.0,
     'L0_ffn_sw3': 8.0}
    for name, (base, spread) in spreads.items():
        noise = np.random.default_rng([zlib.crc32(name.encode()), seed]).standard_normal(out[name].shape)
        drawn = base * np.exp(spread * noise) if base else spread * noise
        out[name] = jnp.asarray(drawn.astype(out[name].dtype))
    for name, factor in factors.items():
        out[name] = (out[name] * factor).astype(out[name].dtype)
    return out
```

```python
from contextlib import ExitStack

import concourse.bass as bass
from concourse import mybir

ALU = mybir.AluOpType
ACT = mybir.ActivationFunctionType
AX = mybir.AxisListType
F32 = mybir.dt.float32
F32R = mybir.dt.float32r

P = 128
SEQS, T, DM = 16, 512, 128
NB = T // P
DI, NS = 256, 16
NC = DI // P
STEPS = NC * NS
E = 8
NE = E + 1
FI = 256
NF = FI // P
UNITS = NE * NF
RING = 4
GROUP = 4
GROUPS = NS // GROUP
G_SLOTS = 3
EPS = 1e-5


def schedule():
    out = [(k, "step", k, "scan") for k in range(STEPS)]
    out += [(0.1, "y_out", 1, "back"), (0.6, "gate_y", 1, "back"), (1.5, "project", 0, "back"),
            (2.2, "moments2", 0, "back"), (3.2, "norm2", 0, "back"), (3.6, "split", 0, "back"),
            (4.4, "route", 0, "back"), (5.2, "rank", 0, "back")]
    first, pace = 4.8, 1.45
    out += [(first + pace * u, "hidden", u, "back") for u in range(UNITS)]
    out += [(first + pace * (NF * e + 1) + 2.1, "expert_out", e, "back") for e in range(NE)]
    out.append((STEPS + 1, "store", 0, "back"))
    out += [(2.4, "delta", 1, "scan"), (2.9, "residual", 0, "scan"), (6.2, "z", 0, "scan"), (7.2, "z", 1, "scan"),
            (17.0, "y_out", 0, "scan"), (18.1, "gate_y", 0, "scan")]
    out += [(0.3, "load_x", 0, "front"), (8.0, "moments1", 0, "front"), (9.1, "norm1", 0, "front"),
            (9.4, "x_t", 0, "front"), (10.0, "x_part", 0, "front"), (10.7, "x_part", 1, "front"),
            (12.2, "bc", 0, "front"), (15.4, "delta", 0, "front"), (18.5, "skip", 0, "front")]
    out += [(20.2 + GROUP * i, "spread", i, "front") for i in range(GROUPS)]
    return out


SCHEDULE = schedule()

MIXED = {"x_t", "x_part", "z", "bc", "delta", "gate_y", "project", "split", "route", "expert_out"}
DELAY = {
    "pe": {"step": 1.6},
    "act": {"x_t": 0.5, "x_part": 0.5, "z": 0.5, "bc": 0.5, "delta": 0.5, "split": 0.5, "rank": 0.4, "hidden": 0.4},
    "dve": {"x_part": 1.1, "z": 1.1, "gate_y": 0.6, "project": 0.6, "split": 1.0, "route": 0.6, "rank": 1.2,
            "hidden": 0.9, "expert_out": 0.6},
    "pool": {"moments2": 0.5, "moments1": 0.5, "hidden": 1.4, "delta": 1.3},
    "sp": {},
}


def pieces(engine, kinds):
    at = [(p + DELAY[engine].get(name, 0), i, name, a, kind)
          for i, (p, name, a, kind) in enumerate(SCHEDULE) if kind in kinds]
    return [(name, a, kind) for _, _, name, a, kind in sorted(at)]


def mixed_jobs(kinds):
    return [(name, a) for name, a, _ in pieces("pe", kinds) if name in MIXED]


FRONT, ALL, LAST, BACK = ("front",), ("front", "scan", "back"), ("scan", "back"), ("back",)
FIRST = ("front", "scan")


def mixed_before(n, kinds):
    if kinds == FRONT:
        return 0
    if kinds == FIRST:
        return len(mixed_jobs(FRONT))
    start = len(mixed_jobs(FRONT)) + len(mixed_jobs(FIRST))
    if kinds == BACK:
        return start + (SEQS - 2) * len(mixed_jobs(ALL)) + len(mixed_jobs(LAST))
    return start + (n - 1) * len(mixed_jobs(ALL))


def kinds_before(n):
    known = {0: FRONT, 1: FIRST, SEQS: LAST}
    return known.get(n, ALL) if isinstance(n, int) else ALL


def mixed_index(n, kinds, name, a):
    return mixed_before(n, kinds) + mixed_jobs(kinds).index((name, a)) + 1


def build(nc, x, w_in, b_in, w_x, b_x, w_dt, b_dt, w_out, b_out, a_log, d_skip,
          gate_w, gate_b, w13, w2, ident_in, below_in, out):
    x_seq = x.rearrange("n (b p) d -> n p b d", p=P)
    out_seq = out.rearrange("n (b p) d -> n p b d", p=P)
    bc_dram = nc.dram_tensor("bc_rows", [2 * NS, T], F32, kind="Internal").ap()

    with ExitStack() as ctx:
        def sb(name, shape, dt=F32):
            return ctx.enter_context(nc.sbuf_tensor(name, shape, dt))

        def bank(name, shape=None):
            return ctx.enter_context(nc.psum_tensor(name, shape or [P, T], F32))

        def sem(name):
            return ctx.enter_context(nc.semaphore(name))

        win_s = sb("win_s", [P, 2 * DI])
        wx_s = sb("wx_s", [P, NC, 2 * NS])
        wdt_s = sb("wdt_s", [P, NC, DI])
        wout_s = sb("wout_s", [P, NC, DM])
        w13_hi = sb("w13_hi", [P, NE * 2 * FI], F32R)
        w13_lo = sb("w13_lo", [P, NE * 2 * FI], F32R)
        w2_s = sb("w2_s", [P, NE, NF, DM])
        gw_s = sb("gw_s", [P, E])
        gb_s = sb("gb_s", [P, E])
        bin_s = sb("bin_s", [P, 4])
        bin_half = sb("bin_half", [P, 4])
        bx_s = sb("bx_s", [2 * NS, 1])
        bdt_s = sb("bdt_s", [P, NC])
        bout_s = sb("bout_s", [P, DM])
        alog_s = sb("alog_s", [P, NC * NS])
        a_exp = sb("a_exp", [P, NC * NS])
        a_neg = sb("a_neg", [P, NC * NS])
        d_s = sb("d_s", [P, NC])
        ident = sb("ident", [P, P])
        below = sb("below", [P, E, E])
        minus_half = sb("minus_half", [P, NB])

        xt = sb("xt", [P, NB, DM])
        stats = sb("stats", [P, NB, 6])
        moments = sb("moments", [P, NB, 2])
        var_eps = sb("var_eps", [P, NB])
        rstd = sb("rstd", [P, NB])
        xnT = sb("xnT", [P, T])
        th_a = sb("th_a", [P, T])
        half_a = sb("half_a", [P, T])
        u = sb("u", [P, NC, T])
        sz = sb("sz", [P, NC, T])
        bc_rows = sb("bc_rows_s", [2 * NS, T])
        soft = sb("soft", [P, T])
        lin = sb("lin", [P, T])
        dt_s = sb("dt_s", [P, NC, T])
        w_s = sb("w_s", [P, NC, T])
        skip = sb("skip", [P, NC, T])
        b_all = sb("b_all", [P, NS, T])
        c_all = sb("c_all", [P, NS, T])
        dbu = sb("dbu", [P, RING, T])
        hc = sb("hc", [P, RING, T])
        y_s = sb("y_s", [P, NB, P])
        res = sb("res", [P, NB, DM])
        acc = sb("acc", [P, NB, DM])
        stats2 = sb("stats2", [P, NB, 6])
        moments2 = sb("moments2", [P, NB, 2])
        var_eps2 = sb("var_eps2", [P, NB])
        rstd2 = sb("rstd2", [P, NB])
        xn2 = sb("xn2", [P, NB, DM])
        x2T = sb("x2T", [P, T])
        x2_hi = sb("x2_hi", [P, T], F32R)
        x2_lo = sb("x2_lo", [P, T], F32R)
        th_b = sb("th_b", [P, T])
        h3_half = sb("h3_half", [P, T])
        q = sb("q", [P, 2, T])
        g = sb("g", [P, G_SLOTS, T])
        top = sb("top", [P, NB])
        shifted = sb("shifted", [P, NB, E])
        expd = sb("expd", [P, NB, E])
        total = sb("total", [P, NB])
        inverse = sb("inverse", [P, NB])
        score = sb("score", [P, NB, E])
        biased = sb("biased", [P, NB, E])
        above = sb("above", [P, NB, E, E])
        tied = sb("tied", [P, NB, E, E])
        rank = sb("rank", [P, NB, E])
        comb = sb("comb", [P, NB, E])

        da = [bank(f"da{i}") for i in range(RING)]
        y_acc = bank("y_acc", [P, NB, P])
        h1 = bank("h1")
        h3 = bank("h3")
        mixed = bank("mixed")
        mixed_blocks = mixed[:, :].rearrange("p (b d) -> p b d", b=NB)

        consts_in = sem("consts_in")
        raw_in = sem("raw_in")
        hi_made = sem("hi_made")
        weights_split = sem("weights_split")
        const_steps = sem("const_steps")
        half_made = sem("half_made")
        half_const = sem("half_const")
        x_in = sem("x_in")
        res_in = sem("res_in")
        rows_out = sem("rows_out")
        spread_in = [sem(f"spread_in{i}") for i in range(GROUPS)]
        stored = sem("stored")
        mixed_written = sem("mixed_written")
        mixed_freed = sem("mixed_freed")
        norm1_steps = sem("norm1_steps")
        rstd1_steps = sem("rstd1_steps")
        silu_made = sem("silu_made")
        soft_steps = sem("soft_steps")
        dt_made = sem("dt_made")
        w_made = sem("w_made")
        skip_made = sem("skip_made")
        decay_made = sem("decay_made")
        dbu_made = sem("dbu_made")
        scanned = sem("scanned")
        hc_made = sem("hc_made")
        reduced = sem("reduced")
        y_copied = sem("y_copied")
        res_biased = sem("res_biased")
        norm2_steps = sem("norm2_steps")
        rstd2_steps = sem("rstd2_steps")
        x2_split = sem("x2_split")
        hidden_made = sem("hidden_made")
        tanh_made = sem("tanh_made")
        h3_copied = sem("h3_copied")
        q_made = sem("q_made")
        g_made = sem("g_made")
        gate_exp = sem("gate_exp")
        route_steps = sem("route_steps")

        passed = sem("passed")

        CONSTS = 15

        def wait(eng, s, value):
            if isinstance(value, int) and value <= 0:
                return
            eng.wait_ge(s, value)

        def wait_apart(eng, s, value):
            eng.wait_ge(s, value)
            eng.sem_inc(passed, 1)

        def pipeline(eng, name, piece):
            def iteration(n, kinds):
                for what, a, kind in pieces(name, kinds):
                    m = n + 1 if kind == "front" else n - 1 if kind == "back" else n
                    piece(what, a, m, n, kinds)

            iteration(-1, FRONT)
            iteration(0, FIRST)
            iteration(1, ALL)
            with eng.Fori(2, SEQS - 1) as n:
                iteration(n, ALL)
            iteration(SEQS - 1, LAST)
            iteration(SEQS, BACK)

        block = ctx.enter_context(nc.Block())

        @block.sync
        def _(sp):
            for dst, src in (
                (win_s[:, :], w_in), (wx_s[:, :, :], w_x), (wdt_s[:, :, :], w_dt), (wout_s[:, :, :], w_out),
                (w2_s[:, :, :, :], w2), (gw_s[:, :], gate_w), (gb_s[:, :], gate_b.partition_broadcast(P)),
                (bin_s[:, :], b_in), (bx_s[:, :], b_x), (bdt_s[:, :], b_dt),
                (bout_s[:, :], b_out.partition_broadcast(P)), (alog_s[:, :], a_log), (d_s[:, :], d_skip),
                (ident[:, :], ident_in), (below[:, :, :], below_in),
            ):
                sp.dma_start(dst, src).then_inc(consts_in, 16)
            half = NE * FI
            for i, raw in enumerate((b_all, c_all)):
                sp.dma_start(raw[:, :, :].rearrange("p s t -> p (s t)")[:, 0:half],
                             w13[:, i * half:(i + 1) * half]).then_inc(raw_in, 16)

            def piece(what, a, m, n, kinds):
                if what == "load_x":
                    if not (isinstance(m, int) and m == 0):
                        wait_apart(sp, mixed_written, mixed_index(n - 1, kinds_before(n), "x_t", 0))
                    sp.dma_start(xt[:, :, :], x_seq[m]).then_inc(x_in, 16)
                elif what == "residual":
                    if not (isinstance(n, int) and n == 0):
                        wait_apart(sp, mixed_freed, mixed_index(n, kinds, "project", 0))
                    sp.dma_start(res[:, :, :], x_seq[m]).then_inc(res_in, 16)
                elif what == "bc":
                    wait_apart(sp, mixed_freed, mixed_index(n, kinds, "bc", 0))
                    for s in spread_in:
                        if not (isinstance(m, int) and m == 0):
                            wait_apart(sp, s, 32 * m)
                    sp.dma_start(bc_dram, bc_rows[:, :]).then_inc(rows_out, 16)
                    wait_apart(sp, rows_out, 16 * (m + 1))
                elif what == "spread":
                    if isinstance(m, int) and m == 0:
                        wait_apart(sp, weights_split, 2)
                    else:
                        last = STEPS * n + NS + GROUP * (a + 1)
                        wait_apart(sp, dbu_made, last)
                        wait_apart(sp, hc_made, last)
                    states = slice(GROUP * a, GROUP * (a + 1))
                    for dst, row in ((b_all, 0), (c_all, NS)):
                        src = bc_dram[row + GROUP * a:row + GROUP * (a + 1), :]
                        sp.dma_start(dst[:, states, :], src.partition_broadcast(P)).then_inc(spread_in[a], 16)
                elif what == "store":
                    wait_apart(sp, mixed_freed, mixed_index(n, kinds, "expert_out", NE - 1))
                    sp.dma_start(out_seq[m], acc[:, :, :]).then_inc(stored, 16)

            pipeline(sp, "sp", piece)
            sp.wait_ge(stored, 16 * SEQS)

        @block.scalar
        def _(act):
            act.wait_ge(consts_in, 16 * CONSTS)
            act.activation(a_exp[:, :], alog_s[:, :], ACT.Exp).then_inc(const_steps, 1)
            act.activation(bin_half[:, :], bin_s[:, :], ACT.Copy, scale=0.5).then_inc(half_made, 1)
            act.wait_ge(const_steps, 1)
            act.activation(a_neg[:, :], a_exp[:, :], ACT.Copy, scale=-1.0).then_inc(const_steps, 1)
            act.wait_ge(half_made, 1)
            act.wait_ge(const_steps, 2)

            def half_and_tanh(m, which, chunk):
                wait(act, silu_made, 4 * m + which)
                act.activation(th_a[:, :], mixed[:, :], ACT.Tanh, bias=bin_half[:, chunk:chunk + 1], scale=0.5)
                act.activation(half_a[:, :], mixed[:, :], ACT.Identity, bias=bin_half[:, chunk:chunk + 1],
                               scale=0.5).then_inc(mixed_freed, 1)

            def piece(what, a, m, n, kinds):
                if what in ("x_t", "x_part", "z", "bc", "delta", "split"):
                    act.wait_ge(mixed_written, mixed_index(n, kinds, what, a))
                if what == "x_t":
                    act.activation(xnT[:, :], mixed[:, :], ACT.Copy).then_inc(mixed_freed, 1)
                elif what == "x_part":
                    half_and_tanh(m, a, a)
                elif what == "z":
                    half_and_tanh(m, 2 + a, 2 + a)
                elif what == "bc":
                    wait(act, rows_out, 16 * m)
                    act.activation(bc_rows[:, :], mixed[0:2 * NS, :], ACT.Identity,
                                   bias=bx_s[:, 0:1]).then_inc(mixed_freed, 1)
                elif what == "delta":
                    wait(act, dt_made, 2 * m + a)
                    bias = bdt_s[:, a:a + 1]
                    done = 6 * m + 3 * a
                    act.activation(soft[:, :], mixed[:, :], ACT.Abs, bias=bias).then_inc(soft_steps, 1)
                    act.activation(lin[:, :], mixed[:, :], ACT.Relu, bias=bias).then_inc(mixed_freed, 1)
                    act.wait_ge(soft_steps, done + 1)
                    act.activation(soft[:, :], soft[:, :], ACT.Exp, scale=-1.0).then_inc(soft_steps, 1)
                    act.wait_ge(soft_steps, done + 2)
                    act.activation(soft[:, :], soft[:, :], ACT.Ln, bias=1.0).then_inc(soft_steps, 1)
                elif what == "skip":
                    act.wait_ge(silu_made, 4 * m + 2)
                    wait(act, reduced, STEPS * (m - 1) + NS + 1)
                    for c in range(NC):
                        act.activation(skip[:, c, :], u[:, c, :], ACT.Copy, scale=d_s[:, c:c + 1]).then_inc(skip_made, 1)
                elif what == "step":
                    c, s = a // NS, a % NS
                    if s == 0:
                        act.wait_ge(dt_made, 2 * m + c + 1)
                    wait(act, hc_made, STEPS * m + a + 1 - RING)
                    col = c * NS + s
                    act.activation(da[a % RING][:, :], dt_s[:, c, :], ACT.Exp,
                                   scale=a_neg[:, col:col + 1]).then_inc(decay_made, 1)
                elif what == "y_out":
                    act.wait_ge(reduced, STEPS * m + NS * (a + 1))
                    if a == 1:
                        before = mixed_index(n - 1, kinds_before(n), "gate_y", 0)
                        act.wait_ge(mixed_written, before)
                    elif not (isinstance(n, int) and n == 0):
                        act.wait_ge(mixed_written, mixed_index(n, kinds, "gate_y", 1))
                    act.activation(y_s[:, :, :], y_acc[:, :, :], ACT.Copy).then_inc(y_copied, 1)
                elif what == "split":
                    act.activation(x2T[:, :], mixed[:, :], ACT.Copy)
                    act.activation(x2_hi[:, :], mixed[:, :], ACT.Copy).then_inc(mixed_freed, 1)
                elif what == "rank":
                    act.wait_ge(mixed_freed, mixed_index(n, kinds, "route", 0))
                    act.activation(expd[:, :, :], shifted[:, :, :], ACT.Exp).then_inc(gate_exp, 1)
                elif what == "hidden":
                    act.wait_ge(hidden_made, 2 * UNITS * m + 2 * a + 1)
                    wait(act, q_made, UNITS * m + a)
                    act.activation(th_b[:, :], h1[:, :], ACT.Tanh, scale=0.5).then_inc(tanh_made, 1)
                    act.wait_ge(hidden_made, 2 * UNITS * m + 2 * a + 2)
                    wait(act, g_made, UNITS * m + a)
                    act.activation(h3_half[:, :], h3[:, :], ACT.Copy, scale=0.5).then_inc(h3_copied, 1)

            pipeline(act, "act", piece)

        @block.gpsimd
        def _(pool):
            pool.memset(minus_half[:, :], -0.5).then_inc(half_const, 1)
            pool.wait_ge(consts_in, 16 * CONSTS)
            pool.wait_ge(half_const, 1)

            def rstd_of(moms, var, r, sems, ready, m):
                wait_apart(pool, ready, 3 * m + 2)
                pool.tensor_scalar(var[:, :], moms[:, :, 1], EPS, None, ALU.add).then_inc(sems, 1)
                pool.wait_ge(sems, 2 * m + 1)
                pool.tensor_tensor(r[:, :], var[:, :], minus_half[:, :], ALU.pow).then_inc(sems, 1)

            def piece(what, a, m, n, kinds):
                if what == "moments1":
                    rstd_of(moments, var_eps, rstd, rstd1_steps, norm1_steps, m)
                elif what == "moments2":
                    rstd_of(moments2, var_eps2, rstd2, rstd2_steps, norm2_steps, m)
                elif what == "residual":
                    pool.wait_ge(res_in, 16 * (m + 1))
                    for b in range(NB):
                        last = pool.tensor_tensor(res[:, b, :], res[:, b, :], bout_s[:, :], ALU.add)
                    last.then_inc(res_biased, 1)
                elif what == "delta":
                    pool.wait_ge(soft_steps, 6 * m + 3 * (a + 1))
                    pool.tensor_tensor(dt_s[:, a, :], soft[:, :], lin[:, :], ALU.add).then_inc(dt_made, 1)
                    pool.wait_ge(dt_made, 2 * m + a + 1)
                    pool.wait_ge(silu_made, 4 * m + a + 1)
                    pool.tensor_tensor(w_s[:, a, :], dt_s[:, a, :], u[:, a, :], ALU.mult).then_inc(w_made, 1)
                elif what == "step":
                    c, s = a // NS, a % NS
                    if s == 0:
                        pool.wait_ge(w_made, 2 * m + c + 1)
                    if c == 0 and s % GROUP == 0:
                        pool.wait_ge(spread_in[s // GROUP], 32 * (m + 1))
                    wait(pool, scanned, STEPS * m + a + 1 - RING)
                    pool.tensor_tensor(dbu[:, a % RING, :], w_s[:, c, :], b_all[:, s, :],
                                       ALU.mult).then_inc(dbu_made, 1)
                elif what == "hidden":
                    pool.wait_ge(q_made, UNITS * m + a + 1)
                    pool.wait_ge(h3_copied, UNITS * m + a + 1)
                    if a >= G_SLOTS:
                        pool.wait_ge(mixed_written, mixed_index(n, kinds, "expert_out", (a - G_SLOTS) // NF))
                    elif not (isinstance(n, int) and n == 1):
                        pool.wait_ge(mixed_written, mixed_index(n - 1, kinds_before(n), "expert_out", (a - G_SLOTS + UNITS) // NF))
                    pool.tensor_tensor(g[:, a % G_SLOTS, :], q[:, a % 2, :], h3_half[:, :],
                                       ALU.mult).then_inc(g_made, 1)

            pipeline(pool, "pool", piece)

        @block.vector
        def _(dve):
            half = NE * FI
            dve.wait_ge(raw_in, 32)
            for i, raw in enumerate((b_all, c_all)):
                flat = raw[:, :, :].rearrange("p s t -> p (s t)")[:, 0:half]
                dve.tensor_copy(w13_hi[:, i * half:(i + 1) * half], flat).then_inc(hi_made, 1)
            for i, raw in enumerate((b_all, c_all)):
                flat = raw[:, :, :].rearrange("p s t -> p (s t)")[:, 0:half]
                dve.wait_ge(hi_made, i + 1)
                dve.tensor_tensor(w13_lo[:, i * half:(i + 1) * half], flat,
                                  w13_hi[:, i * half:(i + 1) * half].bitcast(F32), ALU.subtract).then_inc(weights_split, 1)
            dve.wait_ge(consts_in, 16 * CONSTS)

            def moments_of(src, st, mom, steps, m):
                for b in range(NB):
                    last = dve.bn_stats(st[:, b, :], src[:, b, :])
                last.then_inc(steps, 1)
                wait_apart(dve, steps, 3 * m + 1)
                for b in range(NB):
                    last = dve.bn_aggr(mom[:, b, :], st[:, b, :])
                last.then_inc(steps, 1)

            def normalise(src, dst, mom, r, steps, rsteps, m):
                dve.wait_ge(rsteps, 2 * (m + 1))
                for b in range(NB):
                    last = dve.tensor_scalar(dst[:, b, :], src[:, b, :], mom[:, b, 0:1], r[:, b:b + 1],
                                             ALU.subtract, ALU.mult)
                last.then_inc(steps, 1)

            def multiply_out(k, m):
                c, s = k // NS, k % NS
                dve.wait_ge(scanned, STEPS * m + k + 1)
                if c == 0 and s % GROUP == 0:
                    dve.wait_ge(spread_in[s // GROUP], 32 * (m + 1))
                wait(dve, reduced, STEPS * m + k + 1 - RING)
                dve.tensor_tensor(hc[:, k % RING, :], da[k % RING][:, :], c_all[:, s, :],
                                  ALU.mult).then_inc(hc_made, 1)

            def each_block(ap, inner):
                return ap[:, :, None].broadcast_to([P, NB, inner])

            def piece(what, a, m, n, kinds):
                if what in ("x_part", "z", "gate_y", "project", "route", "expert_out"):
                    if what in ("x_part", "z"):
                        dve.wait_ge(mixed_freed, mixed_index(n, kinds, what, a))
                    else:
                        dve.wait_ge(mixed_written, mixed_index(n, kinds, what, a))
                if what == "moments1":
                    dve.wait_ge(x_in, 16 * (m + 1))
                    moments_of(xt, stats, moments, norm1_steps, m)
                elif what == "norm1":
                    normalise(xt, xt, moments, rstd, norm1_steps, rstd1_steps, m)
                elif what == "x_part":
                    if a == 0:
                        wait(dve, w_made, 2 * m)
                    dve.scalar_tensor_tensor(out=u[:, a, :], in0=th_a[:, :], scalar=1.0, in1=half_a[:, :],
                                             op0=ALU.add, op1=ALU.mult).then_inc(silu_made, 1)
                elif what == "z":
                    dve.scalar_tensor_tensor(out=sz[:, a, :], in0=th_a[:, :], scalar=1.0, in1=half_a[:, :],
                                             op0=ALU.add, op1=ALU.mult).then_inc(silu_made, 1)
                elif what == "step":
                    dve.wait_ge(decay_made, STEPS * m + a + 1)
                    dve.wait_ge(dbu_made, STEPS * m + a + 1)
                    ring = da[a % RING]
                    dve.tensor_tensor_scan(ring[:, :], ring[:, :], dbu[:, a % RING, :], 0.0,
                                           ALU.mult, ALU.add).then_inc(scanned, 1)
                    if a > 0:
                        multiply_out(a - 1, m)
                    if a == STEPS - 1:
                        multiply_out(a, m)
                elif what == "gate_y":
                    dve.wait_ge(silu_made, 4 * m + 3 + a)
                    dve.tensor_tensor(sz[:, a, :], mixed[:, :], sz[:, a, :], ALU.mult).then_inc(mixed_freed, 1)
                elif what == "project":
                    dve.wait_ge(res_biased, m + 1)
                    wait(dve, stored, 16 * m)
                    dve.tensor_tensor(acc[:, :, :], mixed_blocks, res[:, :, :], ALU.add).then_inc(mixed_freed, 1)
                elif what == "moments2":
                    dve.wait_ge(mixed_freed, mixed_index(n, kinds, "project", 0))
                    moments_of(acc, stats2, moments2, norm2_steps, m)
                elif what == "norm2":
                    normalise(acc, xn2, moments2, rstd2, norm2_steps, rstd2_steps, m)
                elif what == "split":
                    dve.wait_ge(mixed_freed, mixed_index(n, kinds, "split", 0))
                    dve.tensor_tensor(x2_lo[:, :], x2T[:, :], x2_hi[:, :].bitcast(F32),
                                      ALU.subtract).then_inc(x2_split, 1)
                elif what == "route":
                    done = 10 * m
                    logits = mixed[:, 0:NB * E].rearrange("p (b e) -> p b e", b=NB)
                    dve.tensor_reduce(top[:, :], logits, AX.X, ALU.max).then_inc(route_steps, 1)
                    dve.wait_ge(route_steps, done + 1)
                    dve.tensor_tensor(shifted[:, :, :], logits, each_block(top, E),
                                      ALU.subtract).then_inc(mixed_freed, 1)
                elif what == "rank":
                    done = 10 * m - 1
                    dve.wait_ge(gate_exp, m + 1)
                    dve.tensor_reduce(total[:, :], expd[:, :, :], AX.X, ALU.add).then_inc(route_steps, 1)
                    dve.wait_ge(route_steps, done + 3)
                    dve.reciprocal(inverse[:, :], total[:, :]).then_inc(route_steps, 1)
                    dve.wait_ge(route_steps, done + 4)
                    dve.tensor_tensor(score[:, :, :], expd[:, :, :], each_block(inverse, E),
                                      ALU.mult).then_inc(route_steps, 1)
                    dve.wait_ge(route_steps, done + 5)
                    dve.tensor_tensor(biased[:, :, :], score[:, :, :],
                                      gb_s[:, None, :].broadcast_to([P, NB, E]), ALU.add).then_inc(route_steps, 1)
                    dve.wait_ge(route_steps, done + 6)
                    other = biased[:, :, None, :].broadcast_to([P, NB, E, E])
                    own = biased[:, :, :, None].broadcast_to([P, NB, E, E])
                    dve.tensor_tensor(above[:, :, :, :], other, own, ALU.is_gt)
                    dve.tensor_tensor(tied[:, :, :, :], other, own, ALU.is_equal).then_inc(route_steps, 1)
                    dve.wait_ge(route_steps, done + 7)
                    dve.tensor_tensor(tied[:, :, :, :], tied[:, :, :, :],
                                      below[:, None, :, :].broadcast_to([P, NB, E, E]), ALU.mult).then_inc(route_steps, 1)
                    dve.wait_ge(route_steps, done + 8)
                    dve.tensor_tensor(above[:, :, :, :], above[:, :, :, :], tied[:, :, :, :],
                                      ALU.add).then_inc(route_steps, 1)
                    dve.wait_ge(route_steps, done + 9)
                    dve.tensor_reduce(rank[:, :, :], above[:, :, :, :], AX.X, ALU.add).then_inc(route_steps, 1)
                    dve.wait_ge(route_steps, done + 10)
                    dve.scalar_tensor_tensor(out=comb[:, :, :], in0=rank[:, :, :], scalar=1.5, in1=score[:, :, :],
                                             op0=ALU.is_lt, op1=ALU.mult).then_inc(route_steps, 1)
                    dve.wait_ge(route_steps, done + 11)
                elif what == "hidden":
                    dve.wait_ge(tanh_made, UNITS * m + a + 1)
                    wait(dve, g_made, UNITS * m + a - 1)
                    dve.scalar_tensor_tensor(out=q[:, a % 2, :], in0=th_b[:, :], scalar=1.0, in1=h1[:, :],
                                             op0=ALU.add, op1=ALU.mult).then_inc(q_made, 1)
                elif what == "expert_out":
                    if a == 0:
                        last = dve.tensor_tensor(acc[:, :, :], mixed_blocks, acc[:, :, :], ALU.add)
                    else:
                        for b in range(NB):
                            last = dve.scalar_tensor_tensor(
                                out=acc[:, b, :], in0=mixed_blocks[:, b, :], scalar=comb[:, b, a - 1:a],
                                in1=acc[:, b, :], op0=ALU.mult, op1=ALU.add)
                    last.then_inc(mixed_freed, 1)

            pipeline(dve, "dve", piece)

        @block.tensor
        def _(pe):
            pe.wait_ge(consts_in, 16 * CONSTS)
            pe.wait_ge(weights_split, 2)

            def w13_at(part, e, which, f):
                at = (e * 2 + which) * FI + f * P
                return part[:, at:at + P]

            def transposes(dst, src):
                for b in range(NB):
                    last = pe.matmul(dst[:, b * P:(b + 1) * P], src(b), ident[:, :], is_transpose=True,
                                     start=(b == 0), stop=(b == NB - 1))
                return last

            def piece(what, a, m, n, kinds):
                if what in MIXED:
                    if what == "x_t":
                        pe.wait_ge(norm1_steps, 3 * (m + 1))
                    elif what == "bc":
                        pe.wait_ge(silu_made, 4 * m + 2)
                    elif what == "gate_y":
                        pe.wait_ge(y_copied, NC * m + a + 1)
                    elif what == "split":
                        pe.wait_ge(norm2_steps, 3 * (m + 1))
                    elif what == "expert_out":
                        pe.wait_ge(g_made, UNITS * m + NF * (a + 1))
                    wait(pe, mixed_freed, mixed_index(n, kinds, what, a) - 1)
                    if what == "x_t":
                        last = transposes(mixed, lambda b: xt[:, b, :])
                    elif what in ("x_part", "z"):
                        col = (a if what == "x_part" else NC + a) * P
                        last = pe.matmul(mixed[:, :], win_s[:, col:col + P], xnT[:, :], start=True, stop=True)
                    elif what == "bc":
                        for c in range(NC):
                            last = pe.matmul(mixed[0:2 * NS, :], wx_s[:, c, :], u[:, c, :],
                                             start=(c == 0), stop=(c == NC - 1))
                    elif what == "delta":
                        for c in range(NC):
                            last = pe.matmul(mixed[:, :], wdt_s[:, c, a * P:(a + 1) * P], u[:, c, :],
                                             start=(c == 0), stop=(c == NC - 1))
                    elif what == "gate_y":
                        last = transposes(mixed, lambda b: y_s[:, b, :])
                    elif what == "project":
                        for b in range(NB):
                            for c in range(NC):
                                last = pe.matmul(mixed_blocks[:, b, :], sz[:, c, b * P:(b + 1) * P], wout_s[:, c, :],
                                                 start=(c == 0), stop=(c == NC - 1))
                    elif what == "split":
                        last = transposes(mixed, lambda b: xn2[:, b, :])
                    elif what == "route":
                        for b in range(NB):
                            last = pe.matmul(mixed[:, b * E:(b + 1) * E], x2T[:, b * P:(b + 1) * P], gw_s[:, :],
                                             start=True, stop=True)
                    elif what == "expert_out":
                        for b in range(NB):
                            for f in range(NF):
                                slot = (NF * a + f) % G_SLOTS
                                last = pe.matmul(mixed_blocks[:, b, :], g[:, slot, b * P:(b + 1) * P],
                                                 w2_s[:, a, f, :], start=(f == 0), stop=(f == NF - 1))
                    last.then_inc(mixed_written, 1)
                elif what == "step":
                    c = a // NS
                    if a % NS == 0:
                        pe.wait_ge(skip_made, NC * (m + 1))
                        wait(pe, y_copied, NC * m + c)
                        for b in range(NB):
                            pe.matmul(y_acc[:, b, :], skip[:, c, b * P:(b + 1) * P], ident[:, :],
                                      is_transpose=True, start=(b == 0), stop=False)
                    pe.wait_ge(hc_made, STEPS * m + a + 1)
                    for b in range(NB):
                        last = pe.matmul(y_acc[:, b, :], hc[:, a % RING, b * P:(b + 1) * P], ident[:, :],
                                         is_transpose=True, start=False, stop=(a % NS == NS - 1 and b == NB - 1))
                    last.then_inc(reduced, 1)
                elif what == "hidden":
                    e, f = a // NF, a % NF
                    if a == 0:
                        pe.wait_ge(x2_split, m + 1)
                    for which, dst, freed in ((0, h1, q_made), (1, h3, h3_copied)):
                        wait(pe, freed, UNITS * m + a)
                        parts = ((w13_hi, x2_hi), (w13_hi, x2_lo), (w13_lo, x2_hi))
                        for i, (w, xx) in enumerate(parts):
                            last = pe.matmul(dst[:, :], w13_at(w, e, which, f), xx[:, :],
                                             start=(i == 0), stop=(i == len(parts) - 1))
                        last.then_inc(hidden_made, 1)

            pipeline(pe, "pe", piece)


INPUTS = ["x", "w_in", "b_in", "w_x", "b_x", "w_dt", "b_dt", "w_out", "b_out", "a_log", "d_skip",
          "gate_w", "gate_b", "w13", "w2", "ident", "below"]


def kernel(**inputs):
    import numpy as np
    import concourse.bacc as bacc
    from concourse.bass_utils import run_bass_kernel_spmd

    a = {k: np.asarray(v) for k, v in inputs.items()}

    def halves(w):
        return w.reshape(NC, P, -1).transpose(1, 0, 2)

    up = np.concatenate([a["L0_ffn_sw1"][None], a["L0_ffn_w1"]])
    lin = np.concatenate([a["L0_ffn_sw3"][None], a["L0_ffn_w3"]])
    down = np.concatenate([a["L0_ffn_sw2"][None], a["L0_ffn_w2"]])
    arrays = {
        "x": a["L0_attn_x"],
        "w_in": a["L0_attn_W_in"],
        "b_in": a["L0_attn_b_in"].reshape(4, P).T,
        "w_x": halves(a["L0_attn_W_xproj"]),
        "b_x": a["L0_attn_b_xproj"][:, None],
        "w_dt": halves(a["L0_attn_W_dt"]),
        "b_dt": a["L0_attn_b_dt"].reshape(NC, P).T,
        "w_out": halves(a["L0_attn_W_out"]),
        "b_out": a["L0_attn_b_out"],
        "a_log": halves(a["L0_attn_A_log"]).reshape(P, NC * NS),
        "d_skip": a["L0_attn_D_param"].reshape(NC, P).T,
        "gate_w": a["L0_ffn_gate_w"].T,
        "gate_b": a["L0_ffn_gate_bias"],
        "w13": np.stack([up, lin], 1).transpose(3, 0, 1, 2).reshape(DM, NE * 2 * FI),
        "w2": down.reshape(NE, DM, NF, P).transpose(3, 0, 2, 1),
        "ident": np.eye(P, dtype=np.float32),
        "below": np.broadcast_to(np.tril(np.ones((E, E), np.float32), -1), (P, E, E)),
    }
    nc = bacc.Bacc("TRN2", target_bir_lowering=False, num_devices=1)
    feeds, aps = {}, []
    for name in INPUTS:
        arr = np.ascontiguousarray(arrays[name])
        feeds[f"in_{name}"] = arr
        aps.append(nc.dram_tensor(f"in_{name}", arr.shape, mybir.dt.from_np(arr.dtype), kind="ExternalInput").ap())
    out = nc.dram_tensor("out_0", (SEQS, T, DM), F32, kind="ExternalOutput").ap()
    build(nc, *aps, out)
    result = run_bass_kernel_spmd(nc, [feeds], core_ids=[0])
    return result.results[0]["out_0"]
```

```python
from contextlib import ExitStack

import concourse.bass as bass
from concourse import mybir

ALU = mybir.AluOpType
ACT = mybir.ActivationFunctionType
AX = mybir.AxisListType
F32 = mybir.dt.float32
F32R = mybir.dt.float32r

P = 128
SEQS, T, DM = 16, 512, 128
NB = T // P
DI, NS = 256, 16
NC = DI // P
STEPS = NC * NS
E = 8
NE = E + 1
FI = 256
NF = FI // P
UNITS = NE * NF
RING = 4
GROUP = 4
GROUPS = NS // GROUP
G_SLOTS = 3
EPS = 1e-5


ORDER = {
    "pe": """
        red.0 gy.1-1 h1.16-2 h3.16-2 proj.0-1 h1.17-2 h3.17-2 red.1 eo.7-2 red.2 red.3 red.4 eo.8-2
        split.0-1 red.5 route.0-1 red.6 red.7 h1.0-1 h3.0-1 red.8 h3.1-1 h1.1-1 red.9 h3.2-1 h1.2-1 eo.0-1
        red.10 h1.3-1 h3.3-1 red.11 z.1 h1.4-1 h3.4-1 x_t.0+1 red.12 h3.5-1 xp.0+1 red.13 h1.5-1 red.14
        eo.1-1 red.15 h1.6-1 h3.6-1 xp.1+1 red.16 h1.7-1 eo.2-1 h3.7-1 red.17 h1.8-1 h3.8-1 bc.0+1 red.18
        red.19 dl.0+1 h1.9-1 h3.9-1 dl.1+1 red.20 h1.10-1 h3.10-1 gy.0 red.21 red.22 red.23 eo.3-1 h1.11-1
        red.24 red.25 red.26 red.27 eo.4-1 h3.11-1 h1.12-1 h3.12-1 z.0+1 red.28 h1.13-1 red.29 eo.5-1
        h3.13-1 h1.14-1 red.30 h3.14-1 red.31 eo.6-1 h1.15-1 h3.15-1
    """,
    "act": """
        decay.0 zcp.0 h3c.12-2 tanh.13-2 decay.1 decay.2 h3c.13-2 decay.3 tanh.14-2 ycopy.1-1 h3c.14-2
        decay.4 decay.5 decay.6 tanh.15-2 h3c.15-2 tanh.16-2 h3c.16-2 decay.7 tanh.17-2 h3c.17-2 decay.8
        splitc.0-1 decay.9 xhi.0-1 decay.10 decay.11 rexp.0-1 tanh.0-1 h3c.0-1 decay.12 tanh.1-1 h3c.1-1
        decay.13 tanh.2-1 h3c.2-1 decay.14 tanh.3-1 decay.15 h3c.3-1 zcp.1 tanh.4-1 h3c.4-1 x_tc.0+1
        decay.16 decay.17 xpc.0+1 decay.18 tanh.5-1 h3c.5-1 decay.19 ycopy.0 tanh.6-1 h3c.6-1 decay.20
        xpc.1+1 decay.21 tanh.7-1 skip.0+1 h3c.7-1 decay.22 tanh.8-1 decay.23 h3c.8-1 bcc.0+1 decay.24
        decay.25 dlc.0+1 tanh.9-1 h3c.9-1 decay.26 decay.27 dlc.1+1 tanh.10-1 soft.0+1 tanh.11-1 decay.28
        h3c.10-1 decay.29 decay.30 decay.31 h3c.11-1 tanh.12-1
    """,
    "dve": """
        scan.0 q.13-2 mul.31-1 comb.5-2 scan.1 mul.0 q.14-2 scan.2 mul.1 mul.2 comb.6-2 q.15-2 gyc.1-1
        scan.3 q.16-2 mul.3 scan.4 projc.0-1 mul.4 q.17-2 mom2.0-1 comb.7-2 scan.5 norm2.0-1 scan.6 comb.8-2
        mul.5 scan.7 mul.6 scan.8 mul.7 xlo.0-1 routec.0-1 scan.9 rank.0-1 mul.8 rank.1-1 q.0-1 rank.2-1
        scan.10 rank.3-1 mul.9 rank.4-1 q.1-1 rank.5-1 scan.11 rank.6-1 mul.10 rank.7-1 q.2-1 rank.8-1
        scan.12 comb.0-1 mul.11 zc.0 q.3-1 scan.13 mul.12 scan.14 zc.1 mul.13 q.4-1 scan.15 mul.14 scan.16
        u.0+1 mul.15 q.5-1 scan.17 comb.1-1 mul.16 q.6-1 scan.18 mul.17 scan.19 u.1+1 mul.18 q.7-1 comb.2-1
        scan.20 mul.19 q.8-1 scan.21 mul.20 scan.22 mul.21 scan.23 mul.22 scan.24 mul.23 scan.25 q.9-1
        scan.26 mom1.0+2 mul.24 gyc.0 q.10-1 mul.25 scan.27 mul.26 comb.3-1 mul.27 norm1.0+2 q.11-1 scan.28
        scan.29 comb.4-1 mul.28 scan.30 q.12-1 mul.29 scan.31 mul.30
    """,
    "pool": """
        dbu.0 dbu.1 g.12-2 dbu.2 g.13-2 dt.1 g.14-2 w.1 dbu.3 g.15-2 dbu.4 g.16-2 dbu.5 dbu.6 g.17-2 rs2.0-1
        dbu.7 dbu.8 dbu.9 dbu.10 dbu.11 dbu.12 dbu.13 g.0-1 dbu.14 g.1-1 dbu.15 g.2-1 dbu.16 g.3-1 dbu.17
        dbu.18 g.4-1 dbu.19 dbu.20 g.5-1 dbu.21 resb.0 g.6-1 dbu.22 dbu.23 g.7-1 dbu.24 g.8-1 dbu.25 dbu.26
        dbu.27 dbu.28 dbu.29 dbu.30 rs1.0+2 dbu.31 g.9-1 dt.0+1 g.10-1 w.0+1 g.11-1
    """,
    "sp": """
        spread.0 spread.1 spread.2 spread.3 store.0-2 loadres.0 load.0+2 rows.0+1
    """,
}


def parsed(text):
    found = []
    for entry in text.split():
        name, rest = entry.split(".")
        arg = rest.replace("-", "+").split("+")[0]
        found.append((name, int(arg), int(rest[len(arg):] or 0)))
    return found


WINDOW = {engine: parsed(text) for engine, text in ORDER.items()}
LEAD = max(off for tasks in WINDOW.values() for _, _, off in tasks)
LAG = -min(off for tasks in WINDOW.values() for _, _, off in tasks)

MIXED = ("x_t", "xp", "z", "bc", "dl", "gy", "proj", "split", "route", "eo")
MIXED_OFFSET = {(name, a): off for name, a, off in WINDOW["pe"] if name in MIXED}
MIXED_ORDER = list(MIXED_OFFSET)


def mixed_uses():
    uses = {}
    for n in range(-LEAD, SEQS + LAG):
        for name, a in MIXED_ORDER:
            m = n + MIXED_OFFSET[name, a]
            if 0 <= m < SEQS:
                uses[name, a, m] = len(uses) + 1
    return uses


MIXED_USES = mixed_uses()


def use_of(name, a, n, off):
    if isinstance(n, int):
        return MIXED_USES.get((name, a, n + off), 0)
    here = MIXED_OFFSET[name, a]
    assert -1 <= off - here <= 0
    return (n + (off - here)) * len(MIXED_ORDER) + MIXED_USES[name, a, LAG + here] - LAG * len(MIXED_ORDER)


def build(nc, x, w_in, b_in, w_x, b_x, w_dt, b_dt, w_out, b_out, a_log, d_skip,
          gate_w, gate_b, w13, w2, ident_in, below_in, out):
    x_seq = x.rearrange("n (b p) d -> n p b d", p=P)
    out_seq = out.rearrange("n (b p) d -> n p b d", p=P)
    bc_dram = nc.dram_tensor("bc_rows", [2 * NS, T], F32, kind="Internal").ap()

    with ExitStack() as ctx:
        def sb(name, shape, dt=F32):
            return ctx.enter_context(nc.sbuf_tensor(name, shape, dt))

        def bank(name, shape=None):
            return ctx.enter_context(nc.psum_tensor(name, shape or [P, T], F32))

        def sem(name):
            return ctx.enter_context(nc.semaphore(name))

        win_s = sb("win_s", [P, 2 * DI])
        wx_s = sb("wx_s", [P, NC, 2 * NS])
        wdt_s = sb("wdt_s", [P, NC, DI])
        wout_s = sb("wout_s", [P, NC, DM])
        w13_hi = sb("w13_hi", [P, NE * 2 * FI], F32R)
        w13_lo = sb("w13_lo", [P, NE * 2 * FI], F32R)
        w2_s = sb("w2_s", [P, NE, NF, DM])
        gw_s = sb("gw_s", [P, E])
        gb_s = sb("gb_s", [P, E])
        bin_s = sb("bin_s", [P, 4])
        bin_half = sb("bin_half", [P, 4])
        bx_s = sb("bx_s", [2 * NS, 1])
        bdt_s = sb("bdt_s", [P, NC])
        bout_s = sb("bout_s", [P, DM])
        alog_s = sb("alog_s", [P, NC * NS])
        a_exp = sb("a_exp", [P, NC * NS])
        a_neg = sb("a_neg", [P, NC * NS])
        d_s = sb("d_s", [P, NC])
        ident = sb("ident", [P, P])
        below = sb("below", [P, E, E])
        minus_half = sb("minus_half", [P, NB])

        xt = sb("xt", [P, NB, DM])
        stats = sb("stats", [P, NB, 6])
        moments = sb("moments", [P, NB, 2])
        var_eps = sb("var_eps", [P, NB])
        rstd = sb("rstd", [P, NB])
        xnT = sb("xnT", [P, T])
        th_a = sb("th_a", [P, T])
        half_a = sb("half_a", [P, T])
        u = sb("u", [P, NC, T])
        sz = sb("sz", [P, NC, T])
        bc_rows = sb("bc_rows_s", [2 * NS, T])
        soft = sb("soft", [P, NC, T])
        lin = sb("lin", [P, NC, T])
        dt_s = sb("dt_s", [P, NC, T])
        w_s = sb("w_s", [P, NC, T])
        skip = sb("skip", [P, NC, T])
        b_all = sb("b_all", [P, NS, T])
        c_all = sb("c_all", [P, NS, T])
        dbu = sb("dbu", [P, RING, T])
        hc = sb("hc", [P, RING, T])
        y_s = sb("y_s", [P, NB, P])
        res = sb("res", [P, NB, DM])
        acc = sb("acc", [P, NB, DM])
        stats2 = sb("stats2", [P, NB, 6])
        moments2 = sb("moments2", [P, NB, 2])
        var_eps2 = sb("var_eps2", [P, NB])
        rstd2 = sb("rstd2", [P, NB])
        xn2 = sb("xn2", [P, NB, DM])
        x2T = sb("x2T", [P, T])
        x2_hi = sb("x2_hi", [P, T], F32R)
        x2_lo = sb("x2_lo", [P, T], F32R)
        th_b = sb("th_b", [P, T])
        h3_half = sb("h3_half", [P, T])
        q = sb("q", [P, 2, T])
        g = sb("g", [P, G_SLOTS, T])
        top = sb("top", [P, NB])
        shifted = sb("shifted", [P, NB, E])
        expd = sb("expd", [P, NB, E])
        total = sb("total", [P, NB])
        inverse = sb("inverse", [P, NB])
        score = sb("score", [P, NB, E])
        biased = sb("biased", [P, NB, E])
        above = sb("above", [P, NB, E, E])
        tied = sb("tied", [P, NB, E, E])
        rank = sb("rank", [P, NB, E])
        comb = sb("comb", [P, NB, E])

        da = [bank(f"da{i}") for i in range(RING)]
        y_acc = bank("y_acc", [P, NB, P])
        h1 = bank("h1")
        h3 = bank("h3")
        mixed = bank("mixed")
        mixed_blocks = mixed[:, :].rearrange("p (b d) -> p b d", b=NB)

        consts_in = sem("consts_in")
        late_in = sem("late_in")
        raw_in = sem("raw_in")
        top_made = sem("top_made")
        hi_made = sem("hi_made")
        weights_split = sem("weights_split")
        const_steps = sem("const_steps")
        half_made = sem("half_made")
        half_const = sem("half_const")
        x_in = sem("x_in")
        res_in = sem("res_in")
        rows_out = sem("rows_out")
        spread_in = [sem(f"spread_in{i}") for i in range(GROUPS)]
        stored = sem("stored")
        mixed_written = sem("mixed_written")
        mixed_freed = sem("mixed_freed")
        norm1_steps = sem("norm1_steps")
        rstd1_steps = sem("rstd1_steps")
        silu_made = sem("silu_made")
        magnitudes = sem("magnitudes")
        soft_steps = sem("soft_steps")
        dt_made = sem("dt_made")
        w_made = sem("w_made")
        skip_made = sem("skip_made")
        decay_made = sem("decay_made")
        dbu_made = sem("dbu_made")
        scanned = sem("scanned")
        hc_made = sem("hc_made")
        reduced = sem("reduced")
        y_copied = sem("y_copied")
        res_biased = sem("res_biased")
        norm2_steps = sem("norm2_steps")
        rstd2_steps = sem("rstd2_steps")
        x2_split = sem("x2_split")
        h1_made = sem("h1_made")
        h3_made = sem("h3_made")
        x2_hi_made = sem("x2_hi_made")
        tanh_made = sem("tanh_made")
        h3_copied = sem("h3_copied")
        q_made = sem("q_made")
        g_made = sem("g_made")
        gate_exp = sem("gate_exp")
        route_steps = sem("route_steps")

        passed = sem("passed")

        CONSTS, LATE, RANK_STEPS = 9, 6, 9

        def wait(eng, s, value):
            if isinstance(value, int) and value <= 0:
                return
            eng.wait_ge(s, value)

        def wait_apart(eng, s, value):
            eng.wait_ge(s, value)
            eng.sem_inc(passed, 1)

        def windows(eng, name, task):
            def window(n):
                for what, a, off in WINDOW[name]:
                    if not isinstance(n, int) or 0 <= n + off < SEQS:
                        task(what, a, n + off, n, off)

            for n in range(-LEAD, LAG + 1):
                window(n)
            with eng.Fori(LAG + 1, SEQS - LEAD) as n:
                window(n)
            for n in range(SEQS - LEAD, SEQS + LAG):
                window(n)

        block = ctx.enter_context(nc.Block())

        stages = [q[:, 0, :], q[:, 1, :], g[:, 0, :], g[:, 1, :], g[:, 2, :], th_b[:, :], h3_half[:, :],
                  xn2[:, :, :].rearrange("p b d -> p (b d)"), acc[:, :, :].rearrange("p b d -> p (b d)")]
        W13 = 2 * FI

        @block.sync
        def _(sp):
            def task(what, a, m, n, off):
                first = isinstance(m, int) and m == 0
                if what == "load":
                    if not first:
                        wait_apart(sp, mixed_written, use_of("x_t", 0, n, off - 1))
                    sp.dma_start(xt[:, :, :], x_seq[m]).then_inc(x_in, 16)
                    if first:
                        load_constants()
                elif what == "loadres":
                    if not first:
                        wait_apart(sp, mixed_freed, use_of("eo", 0, n, off - 1))
                    sp.dma_start(res[:, :, :], x_seq[m]).then_inc(res_in, 16)
                elif what == "rows":
                    wait_apart(sp, mixed_freed, use_of("bc", 0, n, off))
                    if not first:
                        for s in spread_in:
                            wait_apart(sp, s, 32 * m)
                    sp.dma_start(bc_dram, bc_rows[:, :]).then_inc(rows_out, 16)
                elif what == "spread":
                    wait_apart(sp, rows_out, 16 * (m + 1))
                    if not first:
                        last = STEPS * (m - 1) + NS + GROUP * (a + 1)
                        wait_apart(sp, dbu_made, last)
                        wait_apart(sp, hc_made, last)
                    states = slice(GROUP * a, GROUP * (a + 1))
                    for dst, row in ((b_all, 0), (c_all, NS)):
                        src = bc_dram[row + GROUP * a:row + GROUP * (a + 1), :]
                        sp.dma_start(dst[:, states, :], src.partition_broadcast(P)).then_inc(spread_in[a], 16)
                elif what == "store":
                    wait_apart(sp, mixed_freed, use_of("eo", NE - 1, n, off))
                    sp.dma_start(out_seq[m], acc[:, :, :]).then_inc(stored, 16)

            def load_constants():
                for dst, src in (
                    (ident[:, :], ident_in), (bin_s[:, :], b_in), (win_s[:, :], w_in), (bx_s[:, :], b_x),
                    (bdt_s[:, :], b_dt), (alog_s[:, :], a_log), (d_s[:, :], d_skip), (wx_s[:, :, :], w_x),
                    (wdt_s[:, :, :], w_dt),
                ):
                    sp.dma_start(dst, src).then_inc(consts_in, 16)
                for e in range(NE):
                    sp.dma_start(stages[e], w13[:, e * W13:(e + 1) * W13]).then_inc(raw_in, 16)
                for dst, src in (
                    (wout_s[:, :, :], w_out), (bout_s[:, :], b_out.partition_broadcast(P)),
                    (w2_s[:, :, :, :], w2), (gw_s[:, :], gate_w), (gb_s[:, :], gate_b.partition_broadcast(P)),
                    (below[:, :, :], below_in),
                ):
                    sp.dma_start(dst, src).then_inc(late_in, 16)

            windows(sp, "sp", task)
            sp.wait_ge(stored, 16 * SEQS)

        @block.scalar
        def _(act):
            act.wait_ge(consts_in, 16 * CONSTS)
            act.activation(a_exp[:, :], alog_s[:, :], ACT.Exp).then_inc(const_steps, 1)
            act.activation(bin_half[:, :], bin_s[:, :], ACT.Copy, scale=0.5).then_inc(half_made, 1)
            act.wait_ge(const_steps, 1)
            act.activation(a_neg[:, :], a_exp[:, :], ACT.Copy, scale=-1.0).then_inc(const_steps, 1)
            act.wait_ge(half_made, 1)
            act.wait_ge(const_steps, 2)

            def weights_high():
                act.wait_ge(raw_in, 16 * NE)
                for e in range(NE):
                    act.activation(w13_hi[:, e * W13:(e + 1) * W13], stages[e], ACT.Copy).then_inc(hi_made, 1)

            def task(what, a, m, n, off):
                first = isinstance(m, int) and m == 0
                if what in ("x_tc", "xpc", "zcp", "bcc", "dlc", "splitc"):
                    job = {"x_tc": "x_t", "xpc": "xp", "zcp": "z", "bcc": "bc", "dlc": "dl", "splitc": "split"}[what]
                    act.wait_ge(mixed_written, use_of(job, a, n, off))
                if what == "x_tc":
                    act.activation(xnT[:, :], mixed[:, :], ACT.Copy).then_inc(mixed_freed, 1)
                elif what in ("xpc", "zcp"):
                    chunk = a if what == "xpc" else NC + a
                    bias = bin_half[:, chunk:chunk + 1]
                    wait(act, silu_made, 4 * m + chunk)
                    act.activation(th_a[:, :], mixed[:, :], ACT.Tanh, bias=bias, scale=0.5)
                    act.activation(half_a[:, :], mixed[:, :], ACT.Identity, bias=bias, scale=0.5).then_inc(mixed_freed, 1)
                elif what == "bcc":
                    wait(act, rows_out, 16 * m)
                    act.activation(bc_rows[:, :], mixed[0:2 * NS, :], ACT.Identity,
                                   bias=bx_s[:, 0:1]).then_inc(mixed_freed, 1)
                elif what == "dlc":
                    wait(act, dt_made, 2 * (m - 1) + a + 1 if not first else 0)
                    bias = bdt_s[:, a:a + 1]
                    act.activation(soft[:, a, :], mixed[:, :], ACT.Abs, bias=bias).then_inc(magnitudes, 1)
                    act.activation(lin[:, a, :], mixed[:, :], ACT.Relu, bias=bias).then_inc(mixed_freed, 1)
                elif what == "soft":
                    act.wait_ge(magnitudes, NC * (m + 1))
                    act.activation(soft[:, :, :], soft[:, :, :], ACT.Exp, scale=-1.0).then_inc(soft_steps, 1)
                    act.wait_ge(soft_steps, 2 * m + 1)
                    act.activation(soft[:, :, :], soft[:, :, :], ACT.Ln, bias=1.0).then_inc(soft_steps, 1)
                elif what == "skip":
                    act.wait_ge(silu_made, 4 * m + 2)
                    wait(act, reduced, STEPS * (m - 1) + NS + 1)
                    for c in range(NC):
                        act.activation(skip[:, c, :], u[:, c, :], ACT.Copy, scale=d_s[:, c:c + 1]).then_inc(skip_made, 1)
                elif what == "decay":
                    c, s = a // NS, a % NS
                    if s == 0:
                        act.wait_ge(dt_made, 2 * m + c + 1)
                    wait(act, hc_made, STEPS * m + a + 1 - RING)
                    act.activation(da[a % RING][:, :], dt_s[:, c, :], ACT.Exp,
                                   scale=a_neg[:, a:a + 1]).then_inc(decay_made, 1)
                    if first and a == NS - 1:
                        weights_high()
                elif what == "ycopy":
                    act.wait_ge(reduced, STEPS * m + NS * (a + 1))
                    if a == 1:
                        act.wait_ge(mixed_written, use_of("gy", 0, n, off))
                    elif not first:
                        act.wait_ge(mixed_written, use_of("gy", 1, n, off - 1))
                    act.activation(y_s[:, :, :], y_acc[:, :, :], ACT.Copy).then_inc(y_copied, 1)
                elif what == "splitc":
                    act.activation(x2T[:, :], mixed[:, :], ACT.Copy).then_inc(mixed_freed, 1)
                elif what == "xhi":
                    act.wait_ge(mixed_freed, use_of("split", 0, n, off))
                    wait(act, h3_made, UNITS * m)
                    act.activation(x2_hi[:, :], x2T[:, :], ACT.Copy).then_inc(x2_hi_made, 1)
                elif what == "rexp":
                    act.wait_ge(mixed_freed, use_of("route", 0, n, off))
                    act.activation(expd[:, :, :], shifted[:, :, :], ACT.Exp).then_inc(gate_exp, 1)
                elif what == "tanh":
                    act.wait_ge(h1_made, UNITS * m + a + 1)
                    wait(act, q_made, UNITS * m + a)
                    act.activation(th_b[:, :], h1[:, :], ACT.Tanh, scale=0.5).then_inc(tanh_made, 1)
                elif what == "h3c":
                    act.wait_ge(h3_made, UNITS * m + a + 1)
                    wait(act, g_made, UNITS * m + a)
                    act.activation(h3_half[:, :], h3[:, :], ACT.Copy, scale=0.5).then_inc(h3_copied, 1)

            windows(act, "act", task)

        @block.gpsimd
        def _(pool):
            pool.memset(minus_half[:, :], -0.5).then_inc(half_const, 1)
            pool.wait_ge(half_const, 1)

            def rstd_of(moms, var, r, sems, ready, m):
                wait_apart(pool, ready, 3 * m + 2)
                pool.tensor_scalar(var[:, :], moms[:, :, 1], EPS, None, ALU.add).then_inc(sems, 1)
                pool.wait_ge(sems, 2 * m + 1)
                pool.tensor_tensor(r[:, :], var[:, :], minus_half[:, :], ALU.pow).then_inc(sems, 1)

            def task(what, a, m, n, off):
                if what == "rs1":
                    rstd_of(moments, var_eps, rstd, rstd1_steps, norm1_steps, m)
                elif what == "rs2":
                    rstd_of(moments2, var_eps2, rstd2, rstd2_steps, norm2_steps, m)
                elif what == "resb":
                    if isinstance(m, int) and m == 0:
                        pool.wait_ge(late_in, 16 * LATE)
                    pool.wait_ge(res_in, 16 * (m + 1))
                    for b in range(NB):
                        last = pool.tensor_tensor(res[:, b, :], res[:, b, :], bout_s[:, :], ALU.add)
                    last.then_inc(res_biased, 1)
                elif what == "dt":
                    pool.wait_ge(soft_steps, 2 * (m + 1))
                    wait(pool, decay_made, STEPS * (m - 1) + NS * (a + 1))
                    pool.tensor_tensor(dt_s[:, a, :], soft[:, a, :], lin[:, a, :], ALU.add).then_inc(dt_made, 1)
                elif what == "w":
                    pool.wait_ge(dt_made, 2 * m + a + 1)
                    pool.wait_ge(silu_made, 4 * m + a + 1)
                    pool.tensor_tensor(w_s[:, a, :], dt_s[:, a, :], u[:, a, :], ALU.mult).then_inc(w_made, 1)
                elif what == "dbu":
                    c, s = a // NS, a % NS
                    if s == 0:
                        pool.wait_ge(w_made, 2 * m + c + 1)
                    if c == 0 and s % GROUP == 0:
                        pool.wait_ge(spread_in[s // GROUP], 32 * (m + 1))
                    wait(pool, scanned, STEPS * m + a + 1 - RING)
                    pool.tensor_tensor(dbu[:, a % RING, :], w_s[:, c, :], b_all[:, s, :],
                                       ALU.mult).then_inc(dbu_made, 1)
                elif what == "g":
                    pool.wait_ge(q_made, UNITS * m + a + 1)
                    pool.wait_ge(h3_copied, UNITS * m + a + 1)
                    if a >= G_SLOTS:
                        pool.wait_ge(mixed_written, use_of("eo", (a - G_SLOTS) // NF, n, off))
                    elif not (isinstance(m, int) and m == 0):
                        pool.wait_ge(mixed_written, use_of("eo", (a - G_SLOTS + UNITS) // NF, n, off - 1))
                    pool.tensor_tensor(g[:, a % G_SLOTS, :], q[:, a % 2, :], h3_half[:, :],
                                       ALU.mult).then_inc(g_made, 1)

            windows(pool, "pool", task)

        @block.vector
        def _(dve):
            def weights_low():
                for e in range(NE):
                    dve.wait_ge(hi_made, e + 1)
                    hi = w13_hi[:, e * W13:(e + 1) * W13].bitcast(F32)
                    last = dve.tensor_tensor(w13_lo[:, e * W13:(e + 1) * W13], stages[e], hi, ALU.subtract)
                last.then_inc(weights_split, 1)
                dve.wait_ge(weights_split, 1)

            def moments_of(src, st, mom, steps, m):
                for b in range(NB):
                    last = dve.bn_stats(st[:, b, :], src[:, b, :])
                last.then_inc(steps, 1)
                wait_apart(dve, steps, 3 * m + 1)
                for b in range(NB):
                    last = dve.bn_aggr(mom[:, b, :], st[:, b, :])
                last.then_inc(steps, 1)

            def normalise(src, dst, mom, r, steps, rsteps, m):
                dve.wait_ge(rsteps, 2 * (m + 1))
                for b in range(NB):
                    last = dve.tensor_scalar(dst[:, b, :], src[:, b, :], mom[:, b, 0:1], r[:, b:b + 1],
                                             ALU.subtract, ALU.mult)
                last.then_inc(steps, 1)

            def each_block(ap, inner):
                return ap[:, :, None].broadcast_to([P, NB, inner])

            def rank_step(i, m):
                other = biased[:, :, None, :].broadcast_to([P, NB, E, E])
                own = biased[:, :, :, None].broadcast_to([P, NB, E, E])
                if i == 0:
                    dve.wait_ge(gate_exp, m + 1)
                    step = dve.tensor_reduce(total[:, :], expd[:, :, :], AX.X, ALU.add)
                else:
                    dve.wait_ge(route_steps, RANK_STEPS * m + i)
                if i == 1:
                    step = dve.reciprocal(inverse[:, :], total[:, :])
                elif i == 2:
                    step = dve.tensor_tensor(score[:, :, :], expd[:, :, :], each_block(inverse, E), ALU.mult)
                elif i == 3:
                    step = dve.tensor_tensor(biased[:, :, :], score[:, :, :],
                                             gb_s[:, None, :].broadcast_to([P, NB, E]), ALU.add)
                elif i == 4:
                    dve.tensor_tensor(above[:, :, :, :], other, own, ALU.is_gt)
                    step = dve.tensor_tensor(tied[:, :, :, :], other, own, ALU.is_equal)
                elif i == 5:
                    step = dve.tensor_tensor(tied[:, :, :, :], tied[:, :, :, :],
                                             below[:, None, :, :].broadcast_to([P, NB, E, E]), ALU.mult)
                elif i == 6:
                    step = dve.tensor_tensor(above[:, :, :, :], above[:, :, :, :], tied[:, :, :, :], ALU.add)
                elif i == 7:
                    step = dve.tensor_reduce(rank[:, :, :], above[:, :, :, :], AX.X, ALU.add)
                elif i == 8:
                    step = dve.scalar_tensor_tensor(out=comb[:, :, :], in0=rank[:, :, :], scalar=1.5,
                                                    in1=score[:, :, :], op0=ALU.is_lt, op1=ALU.mult)
                step.then_inc(route_steps, 1)

            def task(what, a, m, n, off):
                first = isinstance(m, int) and m == 0
                if what in ("gyc", "projc", "routec", "comb"):
                    job = {"gyc": "gy", "projc": "proj", "routec": "route", "comb": "eo"}[what]
                    dve.wait_ge(mixed_written, use_of(job, a, n, off))
                if what == "mom1":
                    dve.wait_ge(x_in, 16 * (m + 1))
                    moments_of(xt, stats, moments, norm1_steps, m)
                elif what == "norm1":
                    normalise(xt, xt, moments, rstd, norm1_steps, rstd1_steps, m)
                elif what in ("u", "zc"):
                    dve.wait_ge(mixed_freed, use_of("xp" if what == "u" else "z", a, n, off))
                    if what == "u" and a == 0:
                        wait(dve, w_made, 2 * m)
                    dst = u if what == "u" else sz
                    dve.scalar_tensor_tensor(out=dst[:, a, :], in0=th_a[:, :], scalar=1.0, in1=half_a[:, :],
                                             op0=ALU.add, op1=ALU.mult).then_inc(silu_made, 1)
                elif what == "scan":
                    dve.wait_ge(decay_made, STEPS * m + a + 1)
                    dve.wait_ge(dbu_made, STEPS * m + a + 1)
                    ring = da[a % RING]
                    dve.tensor_tensor_scan(ring[:, :], ring[:, :], dbu[:, a % RING, :], 0.0,
                                           ALU.mult, ALU.add).then_inc(scanned, 1)
                elif what == "mul":
                    s = a % NS
                    dve.wait_ge(scanned, STEPS * m + a + 1)
                    if a < NS and s % GROUP == 0:
                        dve.wait_ge(spread_in[s // GROUP], 32 * (m + 1))
                    wait(dve, reduced, STEPS * m + a + 1 - RING)
                    dve.tensor_tensor(hc[:, a % RING, :], da[a % RING][:, :], c_all[:, s, :],
                                      ALU.mult).then_inc(hc_made, 1)
                    if first and a == NS:
                        weights_low()
                elif what == "gyc":
                    dve.wait_ge(silu_made, 4 * m + 3 + a)
                    dve.tensor_tensor(sz[:, a, :], mixed[:, :], sz[:, a, :], ALU.mult).then_inc(mixed_freed, 1)
                elif what == "projc":
                    dve.wait_ge(res_biased, m + 1)
                    dve.tensor_tensor(res[:, :, :], mixed_blocks, res[:, :, :], ALU.add).then_inc(mixed_freed, 1)
                elif what == "mom2":
                    dve.wait_ge(mixed_freed, use_of("proj", 0, n, off))
                    moments_of(res, stats2, moments2, norm2_steps, m)
                elif what == "norm2":
                    if not first:
                        dve.wait_ge(mixed_written, use_of("split", 0, n, off - 1))
                    normalise(res, xn2, moments2, rstd2, norm2_steps, rstd2_steps, m)
                elif what == "xlo":
                    dve.wait_ge(x2_hi_made, m + 1)
                    wait(dve, h3_made, UNITS * m)
                    dve.tensor_tensor(x2_lo[:, :], x2T[:, :], x2_hi[:, :].bitcast(F32),
                                      ALU.subtract).then_inc(x2_split, 1)
                elif what == "routec":
                    logits = mixed[:, 0:NB * E].rearrange("p (b e) -> p b e", b=NB)
                    dve.tensor_reduce(top[:, :], logits, AX.X, ALU.max).then_inc(top_made, 1)
                    dve.wait_ge(top_made, m + 1)
                    dve.tensor_tensor(shifted[:, :, :], logits, each_block(top, E),
                                      ALU.subtract).then_inc(mixed_freed, 1)
                elif what == "rank":
                    rank_step(a, m)
                elif what == "q":
                    dve.wait_ge(tanh_made, UNITS * m + a + 1)
                    wait(dve, g_made, UNITS * m + a - 1)
                    dve.scalar_tensor_tensor(out=q[:, a % 2, :], in0=th_b[:, :], scalar=1.0, in1=h1[:, :],
                                             op0=ALU.add, op1=ALU.mult).then_inc(q_made, 1)
                elif what == "comb":
                    if a == 0:
                        wait(dve, stored, 16 * m)
                        last = dve.tensor_tensor(acc[:, :, :], mixed_blocks, res[:, :, :], ALU.add)
                    else:
                        if a == 1:
                            dve.wait_ge(route_steps, RANK_STEPS * (m + 1))
                        for b in range(NB):
                            last = dve.scalar_tensor_tensor(
                                out=acc[:, b, :], in0=mixed_blocks[:, b, :], scalar=comb[:, b, a - 1:a],
                                in1=acc[:, b, :], op0=ALU.mult, op1=ALU.add)
                    last.then_inc(mixed_freed, 1)

            windows(dve, "dve", task)

        @block.tensor
        def _(pe):
            pe.wait_ge(consts_in, 16 * CONSTS)

            def w13_at(part, e, which, f):
                at = (e * 2 + which) * FI + f * P
                return part[:, at:at + P]

            def transposes(dst, src):
                for b in range(NB):
                    last = pe.matmul(dst[:, b * P:(b + 1) * P], src[:, b, :], ident[:, :], is_transpose=True,
                                     start=(b == 0), stop=(b == NB - 1))
                return last

            def task(what, a, m, n, off):
                first = isinstance(m, int) and m == 0
                if what in MIXED:
                    if what == "x_t":
                        pe.wait_ge(norm1_steps, 3 * (m + 1))
                    elif what in ("bc", "dl"):
                        pe.wait_ge(silu_made, 4 * m + 2)
                    elif what == "gy":
                        pe.wait_ge(y_copied, NC * m + a + 1)
                    elif what == "proj":
                        if first:
                            pe.wait_ge(late_in, 16 * LATE)
                        pe.wait_ge(mixed_freed, use_of("gy", 1, n, off))
                    elif what == "split":
                        pe.wait_ge(norm2_steps, 3 * (m + 1))
                    elif what == "eo":
                        pe.wait_ge(g_made, UNITS * m + NF * (a + 1))
                    wait(pe, mixed_freed, use_of(what, a, n, off) - 1)
                    if what == "x_t":
                        last = transposes(mixed, xt)
                    elif what in ("xp", "z"):
                        col = (a if what == "xp" else NC + a) * P
                        last = pe.matmul(mixed[:, :], win_s[:, col:col + P], xnT[:, :], start=True, stop=True)
                    elif what == "bc":
                        for c in range(NC):
                            last = pe.matmul(mixed[0:2 * NS, :], wx_s[:, c, :], u[:, c, :],
                                             start=(c == 0), stop=(c == NC - 1))
                    elif what == "dl":
                        for c in range(NC):
                            last = pe.matmul(mixed[:, :], wdt_s[:, c, a * P:(a + 1) * P], u[:, c, :],
                                             start=(c == 0), stop=(c == NC - 1))
                    elif what == "gy":
                        last = transposes(mixed, y_s)
                    elif what == "proj":
                        for b in range(NB):
                            for c in range(NC):
                                last = pe.matmul(mixed_blocks[:, b, :], sz[:, c, b * P:(b + 1) * P], wout_s[:, c, :],
                                                 start=(c == 0), stop=(c == NC - 1))
                    elif what == "split":
                        last = transposes(mixed, xn2)
                    elif what == "route":
                        for b in range(NB):
                            last = pe.matmul(mixed[:, b * E:(b + 1) * E], x2T[:, b * P:(b + 1) * P], gw_s[:, :],
                                             start=True, stop=True)
                    elif what == "eo":
                        for b in range(NB):
                            for f in range(NF):
                                slot = (NF * a + f) % G_SLOTS
                                last = pe.matmul(mixed_blocks[:, b, :], g[:, slot, b * P:(b + 1) * P],
                                                 w2_s[:, a, f, :], start=(f == 0), stop=(f == NF - 1))
                    last.then_inc(mixed_written, 1)
                elif what == "red":
                    c = a // NS
                    if a % NS == 0:
                        pe.wait_ge(skip_made, NC * (m + 1))
                        wait(pe, y_copied, NC * m + c)
                        for b in range(NB):
                            pe.matmul(y_acc[:, b, :], skip[:, c, b * P:(b + 1) * P], ident[:, :],
                                      is_transpose=True, start=(b == 0), stop=False)
                    pe.wait_ge(hc_made, STEPS * m + a + 1)
                    for b in range(NB):
                        last = pe.matmul(y_acc[:, b, :], hc[:, a % RING, b * P:(b + 1) * P], ident[:, :],
                                         is_transpose=True, start=False, stop=(a % NS == NS - 1 and b == NB - 1))
                    last.then_inc(reduced, 1)
                elif what in ("h1", "h3"):
                    e, f = a // NF, a % NF
                    if a == 0:
                        if first:
                            pe.wait_ge(weights_split, 1)
                        pe.wait_ge(x2_split, m + 1)
                    which, dst, freed, made = {"h1": (0, h1, q_made, h1_made), "h3": (1, h3, h3_copied, h3_made)}[what]
                    wait(pe, freed, UNITS * m + a)
                    parts = ((w13_hi, x2_hi), (w13_hi, x2_lo), (w13_lo, x2_hi))
                    for i, (w, xx) in enumerate(parts):
                        last = pe.matmul(dst[:, :], w13_at(w, e, which, f), xx[:, :],
                                         start=(i == 0), stop=(i == len(parts) - 1))
                    last.then_inc(made, 1)

            windows(pe, "pe", task)


INPUTS = ["x", "w_in", "b_in", "w_x", "b_x", "w_dt", "b_dt", "w_out", "b_out", "a_log", "d_skip",
          "gate_w", "gate_b", "w13", "w2", "ident", "below"]


def kernel(**inputs):
    import numpy as np
    import concourse.bacc as bacc
    from concourse.bass_utils import run_bass_kernel_spmd

    a = {k: np.asarray(v) for k, v in inputs.items()}

    def halves(w):
        return w.reshape(NC, P, -1).transpose(1, 0, 2)

    up = np.concatenate([a["L0_ffn_sw1"][None], a["L0_ffn_w1"]])
    lin = np.concatenate([a["L0_ffn_sw3"][None], a["L0_ffn_w3"]])
    down = np.concatenate([a["L0_ffn_sw2"][None], a["L0_ffn_w2"]])
    arrays = {
        "x": a["L0_attn_x"],
        "w_in": a["L0_attn_W_in"],
        "b_in": a["L0_attn_b_in"].reshape(4, P).T,
        "w_x": halves(a["L0_attn_W_xproj"]),
        "b_x": a["L0_attn_b_xproj"][:, None],
        "w_dt": halves(a["L0_attn_W_dt"]),
        "b_dt": a["L0_attn_b_dt"].reshape(NC, P).T,
        "w_out": halves(a["L0_attn_W_out"]),
        "b_out": a["L0_attn_b_out"],
        "a_log": halves(a["L0_attn_A_log"]).reshape(P, NC * NS),
        "d_skip": a["L0_attn_D_param"].reshape(NC, P).T,
        "gate_w": a["L0_ffn_gate_w"].T,
        "gate_b": a["L0_ffn_gate_bias"],
        "w13": np.stack([up, lin], 1).transpose(3, 0, 1, 2).reshape(DM, NE * 2 * FI),
        "w2": down.reshape(NE, DM, NF, P).transpose(3, 0, 2, 1),
        "ident": np.eye(P, dtype=np.float32),
        "below": np.broadcast_to(np.tril(np.ones((E, E), np.float32), -1), (P, E, E)),
    }
    nc = bacc.Bacc("TRN2", target_bir_lowering=False, num_devices=1)
    feeds, aps = {}, []
    for name in INPUTS:
        arr = np.ascontiguousarray(arrays[name])
        feeds[f"in_{name}"] = arr
        aps.append(nc.dram_tensor(f"in_{name}", arr.shape, mybir.dt.from_np(arr.dtype), kind="ExternalInput").ap())
    out = nc.dram_tensor("out_0", (SEQS, T, DM), F32, kind="ExternalOutput").ap()
    build(nc, *aps, out)
    result = run_bass_kernel_spmd(nc, [feeds], core_ids=[0])
    return result.results[0]["out_0"]
```

```python
from contextlib import ExitStack

import concourse.bass as bass
from concourse import mybir

ALU = mybir.AluOpType
ACT = mybir.ActivationFunctionType
AX = mybir.AxisListType
F32 = mybir.dt.float32
F32R = mybir.dt.float32r

P = 128
SEQS, T, DM = 16, 512, 128
NB = T // P
DI, NS = 256, 16
NC = DI // P
STEPS = NC * NS
E = 8
NE = E + 1
FI = 256
NF = FI // P
UNITS = NE * NF
RING = 4
GROUP = 4
GROUPS = NS // GROUP
G_SLOTS = 3
EPS = 1e-5
WARM_UP = 4


ORDER = {
    "pe": """
        red.30-1 red.31-1 h1.12-2 h3.12-2 gy.1-1 red.0 h1.13-2 h3.13-2 eo.5-2 h1.14-2 red.1 h3.14-2 proj.0-1
        h1.15-2 h3.15-2 eo.6-2 h3.16-2 h1.16-2 z.0 red.2 red.3 h3.17-2 split.0-1 red.4 h1.17-2 eo.7-2 red.5
        red.6 h1.0-1 route.0-1 h3.0-1 red.7 z.1 h3.1-1 h1.1-1 red.8 eo.8-2 red.9 h3.2-1 h1.2-1 x_t.0+1
        h3.3-1 red.10 xp.0+1 h1.3-1 h3.4-1 red.11 eo.0-1 h1.4-1 red.12 xp.1+1 red.13 h3.5-1 h1.5-1 eo.1-1
        red.14 h1.6-1 red.15 h3.6-1 bc.0+1 red.16 h3.7-1 dl.0+1 red.17 h1.7-1 red.18 red.19 dl.1+1 red.20
        h1.8-1 h3.8-1 gy.0 red.21 red.22 eo.2-1 h1.9-1 red.23 red.24 red.25 red.26 red.27 h3.9-1 h1.10-1
        eo.3-1 h3.10-1 h1.11-1 red.28 red.29 h3.11-1 eo.4-1
    """,
    "act": """
        dlc.0 tanh.7-2 decay.25-1 decay.26-1 decay.27-1 dlc.1 tanh.8-2 soft.0 h3c.8-2 tanh.9-2 sc.2-2
        decay.28-1 decay.29-1 tanh.10-2 h3c.9-2 decay.30-1 sc.3-2 h3c.10-2 decay.31-1 tanh.11-2 decay.0
        h3c.11-2 decay.1 sc.4-2 ycopy.1-1 tanh.12-2 h3c.12-2 decay.2 decay.3 tanh.13-2 h3c.13-2 decay.4
        sc.5-2 tanh.14-2 decay.5 decay.6 h3c.14-2 decay.7 decay.8 tanh.15-2 h3c.15-2 sc.6-2 h3c.16-2
        tanh.16-2 zcp.0 decay.9 splitc.0-1 h3c.17-2 tanh.17-2 xhi.0-1 decay.10 sc.7-2 norm1.0+1 tanh.0-1
        h3c.0-1 rexp.0-1 decay.11 zcp.1 h3c.1-1 tanh.1-1 decay.12 decay.13 sc.8-2 h3c.2-1 tanh.2-1 x_tc.0+1
        decay.14 h3c.3-1 xpc.0+1 tanh.3-1 h3c.4-1 decay.15 decay.16 decay.17 tanh.4-1 decay.18 xpc.1+1
        h3c.5-1 tanh.5-1 decay.19 decay.20 sc.1-1 tanh.6-1 ycopy.0 h3c.6-1 decay.21 decay.22 bcc.0+1
        decay.23 skip.0+1 decay.24 h3c.7-1
    """,
    "dve": """
        scan.2 q.13-2 scan.3 scan.4 mul.2 mul.3 q.14-2 comb.5-2 mul.4 projc.0-1 mom2.0-1 q.15-2 scan.5
        scan.6 mul.5 norm2.0-1 q.16-2 scan.7 comb.6-2 zc.0 mul.6 mul.7 q.17-2 xlo.0-1 scan.8 scan.9 scan.10
        routec.0-1 mul.8 q.0-1 mul.9 comb.7-2 rank.0-1 mul.10 scan.11 rank.1-1 zc.1 q.1-1 rank.2-1 mul.11
        scan.12 comb.8-2 rank.3-1 scan.13 q.2-1 rank.4-1 mul.12 mul.13 scan.14 rank.5-1 q.3-1 u.0+1 rank.6-1
        comb.0-1 mul.14 q.4-1 rank.7-1 scan.15 rank.8-1 scan.16 mul.15 mul.16 q.5-1 u.1+1 scan.17 scan.18
        mul.17 mul.18 scan.19 mul.19 scan.20 scan.21 mul.20 q.6-1 scan.22 mul.21 scan.23 mul.22 mul.23 q.7-1
        mom1.0+2 scan.24 comb.1-1 scan.25 gyc.0 scan.26 mul.24 q.8-1 mul.25 scan.27 mul.26 mul.27 nb.0+2
        dt.0+1 q.9-1 comb.2-1 scan.28 scan.29 q.10-1 mul.28 mul.29 scan.30 comb.3-1 mul.30 scan.31 q.11-1
        mul.31 scan.0+1 dt.1+1 mul.0+1 scan.1+1 q.12-1 comb.4-1 gyc.1 mul.1+1
    """,
    "pool": """
        g.1-2 g.2-2 dbu.15-1 dbu.16-1 dbu.17-1 g.3-2 dbu.18-1 dbu.19-1 dbu.20-1 g.4-2 g.5-2 dbu.21-1
        dbu.22-1 dbu.23-1 g.6-2 dbu.24-1 dbu.25-1 dbu.26-1 dbu.27-1 dbu.28-1 dbu.29-1 dbu.30-1 rs1.0+1 g.7-2
        dbu.31-1 g.8-2 w.0 dbu.0 g.9-2 resb.0-1 g.10-2 dbu.1 g.11-2 dbu.2 dbu.3 dbu.4 g.12-2 g.13-2 dbu.5
        g.14-2 dbu.6 rs2.0-1 dbu.7 dbu.8 g.15-2 dbu.9 dbu.10 g.16-2 dbu.11 dbu.12 g.17-2 dbu.13 g.0-1 dbu.14
        w.1
    """,
    "sp": """
        store.0-2 load.0+2 loadres.0 rows.0+1 spread.0+1 spread.1+1 spread.2+1 spread.3+1
    """,
}


START_ORDER = {
    "pe": """
        x_t.0 warm.0 xp.0 warm.1 xp.1 warm.2 bc.0 dl.0 dl.1 z.0 z.1 red.0 red.1 red.2 warm.3 red.3 x_t.0+1
        red.4 xp.0+1 red.5 red.6 red.7 red.8 xp.1+1 red.9 red.10 red.11 bc.0+1 red.12 red.13 red.14 red.15
        red.16 warm.4 red.17 dl.0+1 red.18 red.19 red.20 dl.1+1 red.21 red.22 red.23 red.24 gy.0 red.25
        red.26 red.27 red.28 red.29
    """,
    "act": """
        norm1.0 x_tc.0 xpc.0 xpc.1 whi.0 whi.1 bcc.0 whi.2 whi.3 dlc.0 skip.0 whi.4 dlc.1 soft.0 zcp.0 whi.5
        decay.0 whi.6 decay.1 whi.7 decay.2 zcp.1 decay.3 norm1.0+1 decay.4 decay.5 decay.6 whi.8 decay.7
        decay.8 decay.9 x_tc.0+1 decay.10 xpc.0+1 decay.11 decay.12 xpc.1+1 decay.13 decay.14 decay.15
        decay.16 decay.17 decay.18 bcc.0+1 decay.19 ycopy.0 decay.20 decay.21 skip.0+1 decay.22 decay.23
        decay.24
    """,
    "dve": """
        mom1.0 nb.0 u.0 u.1 mom1.0+1 wlo.0 wlo.1 nb.0+1 wlo.2 wlo.3 dt.0 wlo.4 zc.0 dt.1 wlo.5 wlo.6 scan.0
        mul.0 scan.1 mul.1 scan.2 zc.1 mul.2 scan.3 scan.4 mul.3 scan.5 mul.4 mul.5 scan.6 scan.7 mul.6
        scan.8 mul.7 mul.8 scan.9 u.0+1 mul.9 scan.10 mul.10 scan.11 u.1+1 mul.11 scan.12 scan.13 mul.12
        mul.13 scan.14 scan.15 mul.14 scan.16 mul.15 mul.16 scan.17 scan.18 mul.17 scan.19 mul.18 scan.20
        mul.19 mul.20 scan.21 scan.22 mul.21 scan.23 mul.22 mul.23 scan.24 scan.25 mul.24 mul.25 mom1.0+2
        wlo.7 scan.26 scan.27 wlo.8 mul.26 gyc.0 mul.27 dt.0+1 scan.28 nb.0+2 scan.29 mul.28 scan.30 mul.29
        scan.31 dt.1+1 mul.30 mul.31 scan.0+1 scan.1+1 mul.0+1 mul.1+1 gyc.1
    """,
    "pool": """
        rs1.0 rs1.0+1 w.0 dbu.0 dbu.1 dbu.2 dbu.3 dbu.4 dbu.5 dbu.6 dbu.7 dbu.8 dbu.9 w.1 dbu.10 dbu.11
        dbu.12 dbu.13 dbu.14
    """,
    "sp": """
        load.0 rows.0 load.0+1 spread.0 spread.1 spread.2 spread.3 load.0+2 rows.0+1 loadres.0 spread.0+1
        spread.1+1 spread.2+1 spread.3+1
    """,
}
END_ORDER = {
    "pe": """
        red.30-1 red.31-1 h1.12-2 h3.12-2 red.0 gy.1-1 h1.13-2 h3.13-2 eo.5-2 h1.14-2 red.1 h3.14-2 proj.0-1
        h3.15-2 red.2 h1.15-2 eo.6-2 red.3 h1.16-2 z.0 h3.16-2 red.4 red.5 split.0-1 h1.17-2 h3.17-2 eo.7-2
        red.6 h3.0-1 red.7 h1.0-1 route.0-1 red.8 h3.1-1 z.1 h1.1-1 h3.2-1 red.9 eo.8-2 red.10 h1.2-1 red.11
        red.12 h3.3-1 red.13 h1.3-1 h3.4-1 red.14 h1.4-1 eo.0-1 red.15 h3.5-1 h1.5-1 eo.1-1 h1.6-1 red.16
        red.17 red.18 h3.6-1 h1.7-1 red.19 h3.7-1 gy.0 red.20 h1.8-1 h3.8-1 eo.2-1 h3.9-1 red.21 h1.9-1
        red.22 red.23 eo.3-1 h3.10-1 h1.10-1 red.24 red.25 h3.11-1 eo.4-1 h1.11-1 red.26 h3.12-1 red.27
        red.28 h1.12-1 red.29 h3.13-1 red.30 red.31 h1.13-1 gy.1 h3.14-1 eo.5-1 h1.14-1 h3.15-1 proj.0
        h1.15-1 h3.16-1 eo.6-1 h1.16-1 h3.17-1 split.0 h1.17-1 eo.7-1 h3.0 h1.0 route.0 h1.1 eo.8-1 h3.1
        h3.2 h1.2 h1.3 h3.3 h3.4 h1.4 h3.5 eo.0 h3.6 h1.5 h1.6 eo.1 h3.7 h1.7 h1.8 eo.2 h3.8 h1.9 h3.9 eo.3
        h1.10 h3.10 h1.11 h3.11 eo.4 h3.12 h3.13 h1.12 h1.13 eo.5 h1.14 h3.14 h1.15 h3.15 eo.6 h3.16 h1.16
        h1.17 h3.17 eo.7 eo.8
    """,
    "act": """
        dlc.0 tanh.7-2 decay.25-1 decay.26-1 decay.27-1 dlc.1 tanh.8-2 soft.0 tanh.9-2 h3c.8-2 sc.2-2
        decay.28-1 decay.29-1 tanh.10-2 h3c.9-2 decay.30-1 sc.3-2 h3c.10-2 decay.31-1 tanh.11-2 h3c.11-2
        decay.0 decay.1 sc.4-2 ycopy.1-1 tanh.12-2 decay.2 decay.3 h3c.12-2 decay.4 tanh.13-2 decay.5
        h3c.13-2 sc.5-2 tanh.14-2 h3c.14-2 decay.6 decay.7 tanh.15-2 h3c.15-2 sc.6-2 decay.8 tanh.16-2 zcp.0
        h3c.16-2 decay.9 splitc.0-1 tanh.17-2 decay.10 xhi.0-1 h3c.17-2 sc.7-2 decay.11 h3c.0-1 decay.12
        tanh.0-1 decay.13 rexp.0-1 h3c.1-1 zcp.1 h3c.2-1 tanh.1-1 decay.14 decay.15 decay.16 tanh.2-1 sc.8-2
        tanh.3-1 h3c.3-1 decay.17 h3c.4-1 tanh.4-1 decay.18 decay.19 tanh.5-1 ycopy.0 h3c.5-1 decay.20
        decay.21 tanh.6-1 sc.1-1 decay.22 h3c.6-1 tanh.7-1 decay.23 h3c.7-1 decay.24 tanh.8-1 decay.25
        h3c.8-1 sc.2-1 decay.26 decay.27 tanh.9-1 decay.28 h3c.9-1 sc.3-1 h3c.10-1 decay.29 tanh.10-1
        decay.30 h3c.11-1 decay.31 tanh.11-1 sc.4-1 h3c.12-1 tanh.12-1 h3c.13-1 ycopy.1 h3c.14-1 tanh.13-1
        sc.5-1 tanh.14-1 h3c.15-1 tanh.15-1 h3c.16-1 sc.6-1 tanh.16-1 splitc.0 xhi.0 h3c.17-1 tanh.17-1
        sc.7-1 rexp.0 h3c.0 tanh.0 tanh.1 sc.8-1 h3c.1 h3c.2 tanh.2 h3c.3 tanh.3 h3c.4 tanh.4 tanh.5 h3c.5
        tanh.6 h3c.6 sc.1 h3c.7 tanh.7 sc.2 tanh.8 tanh.9 h3c.8 h3c.9 sc.3 tanh.10 h3c.10 h3c.11 tanh.11
        sc.4 h3c.12 tanh.12 tanh.13 h3c.13 sc.5 tanh.14 h3c.14 h3c.15 tanh.15 sc.6 h3c.16 tanh.16 tanh.17
        h3c.17 sc.7 sc.8
    """,
    "dve": """
        scan.2 q.13-2 scan.3 mul.2 mul.3 scan.4 scan.5 q.14-2 mul.4 projc.0-1 comb.5-2 mom2.0-1 scan.6
        q.15-2 mul.5 mul.6 scan.7 norm2.0-1 q.16-2 mul.7 comb.6-2 scan.8 scan.9 q.17-2 xlo.0-1 zc.0 mul.8
        scan.10 mul.9 scan.11 routec.0-1 q.0-1 mul.10 rank.0-1 comb.7-2 mul.11 scan.12 scan.13 mul.12 q.1-1
        rank.1-1 scan.14 scan.15 rank.2-1 mul.13 rank.3-1 q.2-1 comb.8-2 mul.14 rank.4-1 scan.16 q.3-1
        mul.15 rank.5-1 scan.17 rank.6-1 q.4-1 scan.18 rank.7-1 comb.0-1 rank.8-1 mul.16 mul.17 q.5-1 mul.18
        scan.19 scan.20 scan.21 q.6-1 mul.19 mul.20 comb.1-1 q.7-1 scan.22 gyc.0 mul.21 scan.23 mul.22
        scan.24 q.8-1 mul.23 comb.2-1 mul.24 scan.25 scan.26 q.9-1 mul.25 mul.26 scan.27 comb.3-1 mul.27
        scan.28 q.10-1 scan.29 mul.28 scan.30 q.11-1 mul.29 scan.31 mul.30 mul.31 q.12-1 zc.1 comb.4-1 gyc.1
        q.13-1 q.14-1 comb.5-1 projc.0 mom2.0 q.15-1 norm2.0 q.16-1 comb.6-1 xlo.0 q.17-1 comb.7-1 routec.0
        q.0 q.1 rank.0 rank.1 comb.8-1 q.2 rank.2 rank.3 rank.4 rank.5 rank.6 rank.7 q.3 q.4 rank.8 comb.0
        q.5 q.6 comb.1 q.7 comb.2 q.8 q.9 comb.3 q.10 q.11 comb.4 q.12 q.13 comb.5 q.14 q.15 comb.6 q.16
        q.17 comb.7 comb.8
    """,
    "pool": """
        g.1-2 g.2-2 dbu.15-1 dbu.16-1 dbu.17-1 g.3-2 dbu.18-1 dbu.19-1 dbu.20-1 g.4-2 g.5-2 dbu.21-1
        resb.0-1 dbu.22-1 dbu.23-1 dbu.24-1 dbu.25-1 g.6-2 dbu.26-1 dbu.27-1 dbu.28-1 dbu.29-1 g.7-2
        dbu.30-1 dbu.31-1 g.8-2 w.0 dbu.0 g.9-2 g.10-2 dbu.1 dbu.2 dbu.3 g.11-2 dbu.4 dbu.5 dbu.6 g.12-2
        g.13-2 g.14-2 dbu.7 dbu.8 rs2.0-1 dbu.9 g.15-2 dbu.10 g.16-2 dbu.11 dbu.12 dbu.13 g.17-2 dbu.14
        g.0-1 w.1 dbu.15 dbu.16 dbu.17 g.1-1 g.2-1 dbu.18 dbu.19 dbu.20 g.3-1 dbu.21 dbu.22 g.4-1 g.5-1
        dbu.23 g.6-1 dbu.24 dbu.25 dbu.26 g.7-1 dbu.27 g.8-1 dbu.28 g.9-1 dbu.29 dbu.30 dbu.31 g.10-1 g.11-1
        g.12-1 resb.0 g.13-1 g.14-1 rs2.0 g.15-1 g.16-1 g.17-1 g.0 g.1 g.2 g.3 g.4 g.5 g.6 g.7 g.8 g.9 g.10
        g.11 g.12 g.13 g.14 g.15 g.16 g.17
    """,
    "sp": """
        store.0-2 loadres.0 store.0-1 store.0
    """,
}


def parsed(text):
    found = []
    for entry in text.split():
        name, rest = entry.split(".")
        arg = rest.replace("-", "+").split("+")[0]
        found.append((name, int(arg), int(rest[len(arg):] or 0)))
    return found


WINDOW = {engine: parsed(text) for engine, text in ORDER.items()}
START = {engine: parsed(text) for engine, text in START_ORDER.items()}
END = {engine: parsed(text) for engine, text in END_ORDER.items()}
LEAD = max(off for tasks in WINDOW.values() for _, _, off in tasks)
LAG = -min(off for tasks in WINDOW.values() for _, _, off in tasks)

MIXED = ("x_t", "xp", "z", "bc", "dl", "gy", "proj", "split", "route", "eo")
MIXED_OFFSET = {(name, a): off for name, a, off in WINDOW["pe"] if name in MIXED}
MIXED_ORDER = list(MIXED_OFFSET)


def mixed_uses():
    tasks = [(name, a, m) for name, a, m in START["pe"]]
    for n in range(1, SEQS - 1):
        tasks += [(name, a, n + off) for name, a, off in WINDOW["pe"] if 0 <= n + off < SEQS]
    tasks += [(name, a, SEQS - 1 + off) for name, a, off in END["pe"]]
    return {task: i + 1 for i, task in enumerate(t for t in tasks if t[0] in MIXED)}


MIXED_USES = mixed_uses()


def use_of(name, a, n, off):
    if isinstance(n, int):
        return MIXED_USES.get((name, a, n + off), 0)
    here = MIXED_OFFSET[name, a]
    assert -1 <= off - here <= LEAD - max(MIXED_OFFSET.values())
    return (n + (off - here)) * len(MIXED_ORDER) + MIXED_USES[name, a, LAG + here] - LAG * len(MIXED_ORDER)


def build(nc, x, w_in, b_in, w_x, b_x, w_dt, b_dt, w_out, b_out, a_log, d_skip,
          gate_w, gate_b, w13, w2, ident_in, below_in, out):
    x_seq = x.rearrange("n (b p) d -> n p b d", p=P)
    out_seq = out.rearrange("n (b p) d -> n p b d", p=P)
    bc_dram = nc.dram_tensor("bc_rows", [2 * NS, T], F32, kind="Internal").ap()

    with ExitStack() as ctx:
        def sb(name, shape, dt=F32):
            return ctx.enter_context(nc.sbuf_tensor(name, shape, dt))

        def bank(name, shape=None):
            return ctx.enter_context(nc.psum_tensor(name, shape or [P, T], F32))

        def sem(name):
            return ctx.enter_context(nc.semaphore(name))

        win_s = sb("win_s", [P, 2 * DI])
        wx_s = sb("wx_s", [P, NC, 2 * NS])
        wdt_s = sb("wdt_s", [P, NC, DI])
        wout_s = sb("wout_s", [P, NC, DM])
        w13_hi = sb("w13_hi", [P, NE * 2 * FI], F32R)
        w13_lo = sb("w13_lo", [P, NE * 2 * FI], F32R)
        w2_s = sb("w2_s", [P, NE, NF, DM])
        gw_s = sb("gw_s", [P, E])
        gb_s = sb("gb_s", [P, E])
        bin_s = sb("bin_s", [P, 4])
        bin_half = sb("bin_half", [P, 4])
        bx_s = sb("bx_s", [2 * NS, 1])
        bdt_s = sb("bdt_s", [P, NC])
        bout_s = sb("bout_s", [P, DM])
        alog_s = sb("alog_s", [P, NC * NS])
        a_exp = sb("a_exp", [P, NC * NS])
        a_neg = sb("a_neg", [P, NC * NS])
        d_s = sb("d_s", [P, NC])
        ident = sb("ident", [P, P])
        below = sb("below", [P, E, E])
        minus_half = sb("minus_half", [P, NB])
        zeros = sb("zeros", [P, 3 * P // 4])

        xt = sb("xt", [P, NB, DM])
        stats = sb("stats", [P, NB, 6])
        moments = sb("moments", [P, NB, 2])
        var_eps = sb("var_eps", [P, NB])
        rstd = sb("rstd", [P, NB])
        shift = sb("shift", [P, NB])
        xnT = sb("xnT", [P, T])
        th_a = sb("th_a", [P, T])
        half_a = sb("half_a", [P, T])
        u = sb("u", [P, NC, T])
        sz = sb("sz", [P, NC, T])
        bc_rows = sb("bc_rows_s", [2 * NS, T])
        soft = sb("soft", [P, NC, T])
        lin = sb("lin", [P, NC, T])
        dt_s = sb("dt_s", [P, NC, T])
        w_s = sb("w_s", [P, NC, T])
        skip = sb("skip", [P, NC, T])
        b_all = sb("b_all", [P, NS, T])
        c_all = sb("c_all", [P, NS, T])
        dbu = sb("dbu", [P, RING, T])
        hc = sb("hc", [P, RING, T])
        y_s = sb("y_s", [P, NB, P])
        res = sb("res", [P, NB, DM])
        acc = sb("acc", [P, NB, DM])
        stats2 = sb("stats2", [P, NB, 6])
        moments2 = sb("moments2", [P, NB, 2])
        var_eps2 = sb("var_eps2", [P, NB])
        rstd2 = sb("rstd2", [P, NB])
        xn2 = sb("xn2", [P, NB, DM])
        x2T = sb("x2T", [P, T])
        x2_hi = sb("x2_hi", [P, T], F32R)
        x2_lo = sb("x2_lo", [P, T], F32R)
        th_b = sb("th_b", [P, 2, T])
        h3_half = sb("h3_half", [P, 2, T])
        q = sb("q", [P, 2, T])
        g = sb("g", [P, G_SLOTS, T])
        top = sb("top", [P, NB])
        shifted = sb("shifted", [P, NB, E])
        expd = sb("expd", [P, NB, E])
        total = sb("total", [P, NB])
        inverse = sb("inverse", [P, NB])
        score = sb("score", [P, NB, E])
        biased = sb("biased", [P, NB, E])
        above = sb("above", [P, NB, E, E])
        tied = sb("tied", [P, NB, E, E])
        rank = sb("rank", [P, NB, E])
        comb = sb("comb", [P, NB, E])
        scaled = sb("scaled", [P, NB, DM])

        da = [bank(f"da{i}") for i in range(RING)]
        y_acc = bank("y_acc", [P, NB, P])
        h1 = bank("h1")
        h3 = bank("h3")
        mixed = bank("mixed")
        mixed_blocks = mixed[:, :].rearrange("p (b d) -> p b d", b=NB)
        spare_blocks = da[2][:, :].rearrange("p (b d) -> p b d", b=NB)

        zeros_made = sem("zeros_made")
        first_in = sem("first_in")
        consts_in = sem("consts_in")
        late_in = sem("late_in")
        raw_in = sem("raw_in")
        top_made = sem("top_made")
        hi_made = sem("hi_made")
        weights_split = sem("weights_split")
        const_steps = sem("const_steps")
        half_made = sem("half_made")
        half_const = sem("half_const")
        x_in = sem("x_in")
        res_in = sem("res_in")
        rows_out = sem("rows_out")
        spread_in = [sem(f"spread_in{i}") for i in range(GROUPS)]
        stored = sem("stored")
        mixed_written = sem("mixed_written")
        mixed_freed = sem("mixed_freed")
        norm1_steps = sem("norm1_steps")
        rstd1_steps = sem("rstd1_steps")
        shift_made = sem("shift_made")
        norm1_made = sem("norm1_made")
        silu_made = sem("silu_made")
        magnitudes = sem("magnitudes")
        soft_steps = sem("soft_steps")
        dt_made = sem("dt_made")
        w_made = sem("w_made")
        skip_made = sem("skip_made")
        decay_made = sem("decay_made")
        dbu_made = sem("dbu_made")
        scanned = sem("scanned")
        hc_made = sem("hc_made")
        reduced = sem("reduced")
        y_copied = sem("y_copied")
        res_biased = sem("res_biased")
        norm2_steps = sem("norm2_steps")
        norm2_made = sem("norm2_made")
        rstd2_steps = sem("rstd2_steps")
        x2_split = sem("x2_split")
        h1_made = sem("h1_made")
        h3_made = sem("h3_made")
        x2_hi_made = sem("x2_hi_made")
        tanh_made = sem("tanh_made")
        h3_copied = sem("h3_copied")
        q_made = sem("q_made")
        g_made = sem("g_made")
        gate_exp = sem("gate_exp")
        route_steps = sem("route_steps")
        combined = sem("combined")

        passed = sem("passed")

        FIRST, CONSTS, LATE, RANK_STEPS = 4, 5, 6, 9

        def wait(eng, s, value):
            if isinstance(value, int) and value <= 0:
                return
            eng.wait_ge(s, value)

        def is_last(m):
            return isinstance(m, int) and m == SEQS - 1

        def unit_banks(a, m):
            return (da[0], da[1]) if is_last(m) and a % 2 else (h1, h3)

        def eo_bank(a, m):
            return spare_blocks if is_last(m) and a % 2 else mixed_blocks

        def wait_apart(eng, s, value):
            eng.wait_ge(s, value)
            eng.sem_inc(passed, 1)

        def windows(eng, name, task):
            def window(n):
                for what, a, off in WINDOW[name]:
                    if not isinstance(n, int) or 0 <= n + off < SEQS:
                        task(what, a, n + off, n, off)

            for what, a, m in START[name]:
                task(what, a, m, 0, m)
            for n in range(1, LAG + 1):
                window(n)
            with eng.Fori(LAG + 1, SEQS - LEAD) as n:
                window(n)
            for n in range(SEQS - LEAD, SEQS - 1):
                window(n)
            for what, a, off in END[name]:
                task(what, a, SEQS - 1 + off, SEQS - 1, off)

        block = ctx.enter_context(nc.Block())

        stages = [q[:, 0, :], q[:, 1, :], g[:, 0, :], g[:, 1, :], g[:, 2, :], th_b[:, 0, :], h3_half[:, 0, :],
                  xn2[:, :, :].rearrange("p b d -> p (b d)"), acc[:, :, :].rearrange("p b d -> p (b d)")]
        W13 = 2 * FI

        @block.sync
        def _(sp):
            def task(what, a, m, n, off):
                first = isinstance(m, int) and m == 0
                if what == "load":
                    if not first:
                        wait_apart(sp, mixed_written, use_of("x_t", 0, n, off - 1))
                    sp.dma_start(xt[:, :, :], x_seq[m]).then_inc(x_in, 16)
                    if first:
                        load_constants()
                elif what == "loadres":
                    if not first:
                        wait_apart(sp, mixed_freed, use_of("eo", 0, n, off - 1))
                    sp.dma_start(res[:, :, :], x_seq[m]).then_inc(res_in, 16)
                elif what == "rows":
                    wait_apart(sp, mixed_freed, use_of("bc", 0, n, off))
                    if not first:
                        for s in spread_in:
                            wait_apart(sp, s, 32 * m)
                    sp.dma_start(bc_dram, bc_rows[:, :]).then_inc(rows_out, 16)
                elif what == "spread":
                    wait_apart(sp, rows_out, 16 * (m + 1))
                    if not first:
                        last = STEPS * (m - 1) + NS + GROUP * (a + 1)
                        wait_apart(sp, dbu_made, last)
                        wait_apart(sp, hc_made, last)
                    states = slice(GROUP * a, GROUP * (a + 1))
                    for dst, row in ((b_all, 0), (c_all, NS)):
                        src = bc_dram[row + GROUP * a:row + GROUP * (a + 1), :]
                        sp.dma_start(dst[:, states, :], src.partition_broadcast(P)).then_inc(spread_in[a], 16)
                elif what == "store":
                    wait_apart(sp, combined, E * (m + 1))
                    sp.dma_start(out_seq[m], acc[:, :, :]).then_inc(stored, 16)

            def load_constants():
                for dst, src in (
                    (bin_s[:, :], b_in), (alog_s[:, :], a_log), (ident[:, :], ident_in), (win_s[:, :], w_in),
                ):
                    sp.dma_start(dst, src).then_inc(first_in, 16)
                for dst, src in (
                    (bx_s[:, :], b_x), (bdt_s[:, :], b_dt), (d_s[:, :], d_skip), (wx_s[:, :, :], w_x),
                    (wdt_s[:, :, :], w_dt),
                ):
                    sp.dma_start(dst, src).then_inc(consts_in, 16)
                for e in range(NE):
                    sp.dma_start(stages[e], w13[:, e * W13:(e + 1) * W13]).then_inc(raw_in, 16)
                for dst, src in (
                    (wout_s[:, :, :], w_out), (bout_s[:, :], b_out.partition_broadcast(P)),
                    (w2_s[:, :, :, :], w2), (gw_s[:, :], gate_w), (gb_s[:, :], gate_b.partition_broadcast(P)),
                    (below[:, :, :], below_in),
                ):
                    sp.dma_start(dst, src).then_inc(late_in, 16)

            windows(sp, "sp", task)
            sp.wait_ge(stored, 16 * SEQS)

        @block.scalar
        def _(act):
            act.wait_ge(first_in, 16 * FIRST)
            act.activation(a_exp[:, :], alog_s[:, :], ACT.Exp).then_inc(const_steps, 1)
            act.activation(bin_half[:, :], bin_s[:, :], ACT.Copy, scale=0.5).then_inc(half_made, 1)
            act.wait_ge(const_steps, 1)
            act.activation(a_neg[:, :], a_exp[:, :], ACT.Copy, scale=-1.0).then_inc(const_steps, 1)
            act.wait_ge(half_made, 1)
            act.wait_ge(const_steps, 2)

            def task(what, a, m, n, off):
                first = isinstance(m, int) and m == 0
                if first and what in ("bcc", "dlc", "skip"):
                    act.wait_ge(consts_in, 16 * CONSTS)
                if what in ("x_tc", "xpc", "zcp", "bcc", "dlc", "splitc", "sc"):
                    job = {"x_tc": "x_t", "xpc": "xp", "zcp": "z", "bcc": "bc", "dlc": "dl", "splitc": "split",
                           "sc": "eo"}[what]
                    act.wait_ge(mixed_written, use_of(job, a, n, off))
                if what == "whi":
                    if a == 0:
                        act.wait_ge(raw_in, 16 * NE)
                    act.activation(w13_hi[:, a * W13:(a + 1) * W13], stages[a], ACT.Copy).then_inc(hi_made, 1)
                elif what == "norm1":
                    act.wait_ge(shift_made, m + 1)
                    for b in range(NB):
                        last = act.activation(xt[:, b, :], xt[:, b, :], ACT.Identity,
                                              bias=shift[:, b:b + 1], scale=rstd[:, b:b + 1])
                    last.then_inc(norm1_made, 1)
                elif what == "x_tc":
                    act.activation(xnT[:, :], mixed[:, :], ACT.Copy).then_inc(mixed_freed, 1)
                elif what in ("xpc", "zcp"):
                    chunk = a if what == "xpc" else NC + a
                    bias = bin_half[:, chunk:chunk + 1]
                    wait(act, silu_made, 4 * m + chunk)
                    act.activation(th_a[:, :], mixed[:, :], ACT.Tanh, bias=bias, scale=0.5)
                    act.activation(half_a[:, :], mixed[:, :], ACT.Identity, bias=bias, scale=0.5).then_inc(mixed_freed, 1)
                elif what == "bcc":
                    wait(act, rows_out, 16 * m)
                    act.activation(bc_rows[:, :], mixed[0:2 * NS, :], ACT.Identity,
                                   bias=bx_s[:, 0:1]).then_inc(mixed_freed, 1)
                elif what == "dlc":
                    wait(act, dt_made, 2 * (m - 1) + a + 1 if not first else 0)
                    bias = bdt_s[:, a:a + 1]
                    act.activation(soft[:, a, :], mixed[:, :], ACT.Abs, bias=bias).then_inc(magnitudes, 1)
                    act.activation(lin[:, a, :], mixed[:, :], ACT.Relu, bias=bias).then_inc(mixed_freed, 1)
                elif what == "soft":
                    act.wait_ge(magnitudes, NC * (m + 1))
                    act.activation(soft[:, :, :], soft[:, :, :], ACT.Exp, scale=-1.0).then_inc(soft_steps, 1)
                    act.wait_ge(soft_steps, 2 * m + 1)
                    act.activation(soft[:, :, :], soft[:, :, :], ACT.Ln, bias=1.0).then_inc(soft_steps, 1)
                elif what == "skip":
                    act.wait_ge(silu_made, 4 * m + 2)
                    wait(act, reduced, STEPS * (m - 1) + NS + 1)
                    for c in range(NC):
                        act.activation(skip[:, c, :], u[:, c, :], ACT.Copy, scale=d_s[:, c:c + 1]).then_inc(skip_made, 1)
                elif what == "decay":
                    c, s = a // NS, a % NS
                    if s == 0:
                        act.wait_ge(dt_made, 2 * m + c + 1)
                    wait(act, hc_made, STEPS * m + a + 1 - RING)
                    act.activation(da[a % RING][:, :], dt_s[:, c, :], ACT.Exp,
                                   scale=a_neg[:, a:a + 1]).then_inc(decay_made, 1)
                elif what == "ycopy":
                    act.wait_ge(reduced, STEPS * m + NS * (a + 1))
                    if a == 1:
                        act.wait_ge(mixed_written, use_of("gy", 0, n, off))
                    elif not first:
                        act.wait_ge(mixed_written, use_of("gy", 1, n, off - 1))
                    act.activation(y_s[:, :, :], y_acc[:, :, :], ACT.Copy).then_inc(y_copied, 1)
                elif what == "splitc":
                    act.activation(x2T[:, :], mixed[:, :], ACT.Copy).then_inc(mixed_freed, 1)
                elif what == "xhi":
                    act.wait_ge(mixed_freed, use_of("split", 0, n, off))
                    wait(act, h1_made, UNITS * m)
                    wait(act, h3_made, UNITS * m)
                    act.activation(x2_hi[:, :], x2T[:, :], ACT.Copy).then_inc(x2_hi_made, 1)
                elif what == "rexp":
                    act.wait_ge(mixed_freed, use_of("route", 0, n, off))
                    act.activation(expd[:, :, :], shifted[:, :, :], ACT.Exp).then_inc(gate_exp, 1)
                elif what == "tanh":
                    act.wait_ge(h1_made, UNITS * m + a + 1)
                    wait(act, q_made, UNITS * m + a - 1)
                    act.activation(th_b[:, a % 2, :], unit_banks(a, m)[0][:, :], ACT.Tanh, scale=0.5).then_inc(tanh_made, 1)
                elif what == "h3c":
                    act.wait_ge(h3_made, UNITS * m + a + 1)
                    wait(act, g_made, UNITS * m + a - 1)
                    act.activation(h3_half[:, a % 2, :], unit_banks(a, m)[1][:, :], ACT.Copy, scale=0.5).then_inc(h3_copied, 1)
                elif what == "sc":
                    if a == 1:
                        act.wait_ge(route_steps, RANK_STEPS * (m + 1))
                        act.wait_ge(mixed_freed, use_of("eo", 0, n, off))
                    wait(act, combined, E * m + a - 1)
                    for b in range(NB):
                        last = act.activation(scaled[:, b, :], eo_bank(a, m)[:, b, :], ACT.Copy,
                                              scale=comb[:, b, a - 1:a])
                    last.then_inc(mixed_freed, 1)

            windows(act, "act", task)

        @block.gpsimd
        def _(pool):
            pool.memset(zeros[:, :], 0.0).then_inc(zeros_made, 1)
            pool.memset(minus_half[:, :], -0.5).then_inc(half_const, 1)
            pool.wait_ge(half_const, 1)

            def rstd_of(moms, var, r, sems, ready, m):
                wait_apart(pool, ready, 2 * m + 2)
                pool.tensor_scalar(var[:, :], moms[:, :, 1], EPS, None, ALU.add).then_inc(sems, 1)
                pool.wait_ge(sems, 2 * m + 1)
                pool.tensor_tensor(r[:, :], var[:, :], minus_half[:, :], ALU.pow).then_inc(sems, 1)

            def task(what, a, m, n, off):
                if what == "rs1":
                    rstd_of(moments, var_eps, rstd, rstd1_steps, norm1_steps, m)
                elif what == "rs2":
                    rstd_of(moments2, var_eps2, rstd2, rstd2_steps, norm2_steps, m)
                elif what == "resb":
                    if isinstance(m, int) and m == 0:
                        pool.wait_ge(late_in, 16 * LATE)
                    pool.wait_ge(res_in, 16 * (m + 1))
                    pool.tensor_tensor(res[:, :, :], res[:, :, :], bout_s[:, None, :].broadcast_to([P, NB, DM]),
                                       ALU.add).then_inc(res_biased, 1)
                elif what == "w":
                    pool.wait_ge(dt_made, 2 * m + a + 1)
                    pool.wait_ge(silu_made, 4 * m + a + 1)
                    pool.tensor_tensor(w_s[:, a, :], dt_s[:, a, :], u[:, a, :], ALU.mult).then_inc(w_made, 1)
                elif what == "dbu":
                    c, s = a // NS, a % NS
                    if s == 0:
                        pool.wait_ge(w_made, 2 * m + c + 1)
                    if c == 0 and s % GROUP == 0:
                        pool.wait_ge(spread_in[s // GROUP], 32 * (m + 1))
                    wait(pool, scanned, STEPS * m + a + 1 - RING)
                    pool.tensor_tensor(dbu[:, a % RING, :], w_s[:, c, :], b_all[:, s, :],
                                       ALU.mult).then_inc(dbu_made, 1)
                elif what == "g":
                    pool.wait_ge(q_made, UNITS * m + a + 1)
                    pool.wait_ge(h3_copied, UNITS * m + a + 1)
                    if a >= G_SLOTS:
                        pool.wait_ge(mixed_written, use_of("eo", (a - G_SLOTS) // NF, n, off))
                    elif not (isinstance(m, int) and m == 0):
                        pool.wait_ge(mixed_written, use_of("eo", (a - G_SLOTS + UNITS) // NF, n, off - 1))
                    pool.tensor_tensor(g[:, a % G_SLOTS, :], q[:, a % 2, :], h3_half[:, a % 2, :],
                                       ALU.mult).then_inc(g_made, 1)

            windows(pool, "pool", task)

        @block.vector
        def _(dve):
            def moments_of(src, st, mom, steps, m):
                for b in range(NB):
                    last = dve.bn_stats(st[:, b, :], src[:, b, :])
                last.then_inc(steps, 1)
                wait_apart(dve, steps, 2 * m + 1)
                for b in range(NB):
                    last = dve.bn_aggr(mom[:, b, :], st[:, b, :])
                last.then_inc(steps, 1)

            def each_block(ap, inner):
                return ap[:, :, None].broadcast_to([P, NB, inner])

            def rank_step(i, m):
                other = biased[:, :, None, :].broadcast_to([P, NB, E, E])
                own = biased[:, :, :, None].broadcast_to([P, NB, E, E])
                if i == 0:
                    dve.wait_ge(gate_exp, m + 1)
                    step = dve.tensor_reduce(total[:, :], expd[:, :, :], AX.X, ALU.add)
                else:
                    dve.wait_ge(route_steps, RANK_STEPS * m + i)
                if i == 1:
                    step = dve.reciprocal(inverse[:, :], total[:, :])
                elif i == 2:
                    step = dve.tensor_tensor(score[:, :, :], expd[:, :, :], each_block(inverse, E), ALU.mult)
                elif i == 3:
                    step = dve.tensor_tensor(biased[:, :, :], score[:, :, :],
                                             gb_s[:, None, :].broadcast_to([P, NB, E]), ALU.add)
                elif i == 4:
                    dve.tensor_tensor(above[:, :, :, :], other, own, ALU.is_gt)
                    step = dve.tensor_tensor(tied[:, :, :, :], other, own, ALU.is_equal)
                elif i == 5:
                    step = dve.tensor_tensor(tied[:, :, :, :], tied[:, :, :, :],
                                             below[:, None, :, :].broadcast_to([P, NB, E, E]), ALU.mult)
                elif i == 6:
                    step = dve.tensor_tensor(above[:, :, :, :], above[:, :, :, :], tied[:, :, :, :], ALU.add)
                elif i == 7:
                    step = dve.tensor_reduce(rank[:, :, :], above[:, :, :, :], AX.X, ALU.add)
                elif i == 8:
                    step = dve.scalar_tensor_tensor(out=comb[:, :, :], in0=rank[:, :, :], scalar=1.5,
                                                    in1=score[:, :, :], op0=ALU.is_lt, op1=ALU.mult)
                step.then_inc(route_steps, 1)

            def task(what, a, m, n, off):
                first = isinstance(m, int) and m == 0
                if what in ("gyc", "projc", "routec") or (what, a) == ("comb", 0):
                    job = {"gyc": "gy", "projc": "proj", "routec": "route", "comb": "eo"}[what]
                    dve.wait_ge(mixed_written, use_of(job, a, n, off))
                if what == "wlo":
                    dve.wait_ge(hi_made, a + 1)
                    hi = w13_hi[:, a * W13:(a + 1) * W13].bitcast(F32)
                    dve.tensor_tensor(w13_lo[:, a * W13:(a + 1) * W13], stages[a], hi,
                                      ALU.subtract).then_inc(weights_split, 1)
                elif what == "mom1":
                    dve.wait_ge(x_in, 16 * (m + 1))
                    moments_of(xt, stats, moments, norm1_steps, m)
                elif what == "nb":
                    dve.wait_ge(rstd1_steps, 2 * (m + 1))
                    dve.scalar_tensor_tensor(out=shift[:, :], in0=moments[:, :, 0], scalar=-1.0, in1=rstd[:, :],
                                             op0=ALU.mult, op1=ALU.mult).then_inc(shift_made, 1)
                elif what == "dt":
                    dve.wait_ge(soft_steps, 2 * (m + 1))
                    wait(dve, decay_made, STEPS * (m - 1) + NS * (a + 1))
                    wait(dve, w_made, 2 * (m - 1) + a + 1)
                    dve.tensor_tensor(dt_s[:, a, :], soft[:, a, :], lin[:, a, :], ALU.add).then_inc(dt_made, 1)
                elif what in ("u", "zc"):
                    dve.wait_ge(mixed_freed, use_of("xp" if what == "u" else "z", a, n, off))
                    if what == "u" and a == 0:
                        wait(dve, w_made, 2 * m)
                    dst = u if what == "u" else sz
                    dve.scalar_tensor_tensor(out=dst[:, a, :], in0=th_a[:, :], scalar=1.0, in1=half_a[:, :],
                                             op0=ALU.add, op1=ALU.mult).then_inc(silu_made, 1)
                elif what == "scan":
                    dve.wait_ge(decay_made, STEPS * m + a + 1)
                    dve.wait_ge(dbu_made, STEPS * m + a + 1)
                    ring = da[a % RING]
                    dve.tensor_tensor_scan(ring[:, :], ring[:, :], dbu[:, a % RING, :], 0.0,
                                           ALU.mult, ALU.add).then_inc(scanned, 1)
                elif what == "mul":
                    s = a % NS
                    dve.wait_ge(scanned, STEPS * m + a + 1)
                    if a < NS and s % GROUP == 0:
                        dve.wait_ge(spread_in[s // GROUP], 32 * (m + 1))
                    wait(dve, reduced, STEPS * m + a + 1 - RING)
                    dve.tensor_tensor(hc[:, a % RING, :], da[a % RING][:, :], c_all[:, s, :],
                                      ALU.mult).then_inc(hc_made, 1)
                elif what == "gyc":
                    dve.wait_ge(silu_made, 4 * m + 3 + a)
                    dve.tensor_tensor(sz[:, a, :], mixed[:, :], sz[:, a, :], ALU.mult).then_inc(mixed_freed, 1)
                elif what == "projc":
                    dve.wait_ge(res_biased, m + 1)
                    dve.tensor_tensor(res[:, :, :], mixed_blocks, res[:, :, :], ALU.add).then_inc(mixed_freed, 1)
                elif what == "mom2":
                    dve.wait_ge(mixed_freed, use_of("proj", 0, n, off))
                    moments_of(res, stats2, moments2, norm2_steps, m)
                elif what == "norm2":
                    if first:
                        dve.wait_ge(weights_split, NE)
                    else:
                        dve.wait_ge(mixed_written, use_of("split", 0, n, off - 1))
                    dve.wait_ge(rstd2_steps, 2 * (m + 1))
                    for b in range(NB):
                        last = dve.tensor_scalar(xn2[:, b, :], res[:, b, :], moments2[:, b, 0:1], rstd2[:, b:b + 1],
                                                 ALU.subtract, ALU.mult)
                    last.then_inc(norm2_made, 1)
                elif what == "xlo":
                    dve.wait_ge(x2_hi_made, m + 1)
                    wait(dve, h1_made, UNITS * m)
                    wait(dve, h3_made, UNITS * m)
                    dve.tensor_tensor(x2_lo[:, :], x2T[:, :], x2_hi[:, :].bitcast(F32),
                                      ALU.subtract).then_inc(x2_split, 1)
                elif what == "routec":
                    logits = mixed[:, 0:NB * E].rearrange("p (b e) -> p b e", b=NB)
                    dve.tensor_reduce(top[:, :], logits, AX.X, ALU.max).then_inc(top_made, 1)
                    dve.wait_ge(top_made, m + 1)
                    dve.tensor_tensor(shifted[:, :, :], logits, each_block(top, E),
                                      ALU.subtract).then_inc(mixed_freed, 1)
                elif what == "rank":
                    rank_step(a, m)
                elif what == "q":
                    dve.wait_ge(tanh_made, UNITS * m + a + 1)
                    wait(dve, g_made, UNITS * m + a - 1)
                    dve.scalar_tensor_tensor(out=q[:, a % 2, :], in0=th_b[:, a % 2, :], scalar=1.0,
                                             in1=unit_banks(a, m)[0][:, :],
                                             op0=ALU.add, op1=ALU.mult).then_inc(q_made, 1)
                elif what == "comb":
                    if a == 0:
                        wait(dve, stored, 16 * m)
                        dve.tensor_tensor(acc[:, :, :], mixed_blocks, res[:, :, :], ALU.add).then_inc(mixed_freed, 1)
                    else:
                        dve.wait_ge(mixed_freed, use_of("eo", a, n, off))
                        dve.tensor_tensor(acc[:, :, :], acc[:, :, :], scaled[:, :, :], ALU.add).then_inc(combined, 1)

            windows(dve, "dve", task)

        @block.tensor
        def _(pe):
            def warm():
                for b in range(NB):
                    pe.matmul(h1[0:3 * P // 4, b * P:b * P + 3 * P // 4], zeros[:, :], zeros[:, :], start=True, stop=True)

            pe.wait_ge(zeros_made, 1)
            for _ in range(WARM_UP):
                warm()
            pe.wait_ge(first_in, 16 * FIRST)

            def w13_at(part, e, which, f):
                at = (e * 2 + which) * FI + f * P
                return part[:, at:at + P]

            def transposes(dst, src):
                for b in range(NB):
                    last = pe.matmul(dst[:, b * P:(b + 1) * P], src[:, b, :], ident[:, :], is_transpose=True,
                                     start=(b == 0), stop=(b == NB - 1))
                return last

            def task(what, a, m, n, off):
                first = isinstance(m, int) and m == 0
                if what == "warm":
                    warm()
                if what in MIXED:
                    if what == "x_t":
                        pe.wait_ge(norm1_made, m + 1)
                    elif what in ("bc", "dl"):
                        if first:
                            pe.wait_ge(consts_in, 16 * CONSTS)
                        pe.wait_ge(silu_made, 4 * m + 2)
                    elif what == "gy":
                        pe.wait_ge(y_copied, NC * m + a + 1)
                    elif what == "proj":
                        if first:
                            pe.wait_ge(late_in, 16 * LATE)
                        pe.wait_ge(mixed_freed, use_of("gy", 1, n, off))
                    elif what == "split":
                        pe.wait_ge(norm2_made, m + 1)
                    elif what == "eo":
                        pe.wait_ge(g_made, UNITS * m + NF * (a + 1))
                    alternates = what == "eo" and a > 0 and is_last(m)
                    wait(pe, mixed_freed, use_of(what, a, n, off) - (2 if alternates else 1))
                    if what == "x_t":
                        last = transposes(mixed, xt)
                    elif what in ("xp", "z"):
                        col = (a if what == "xp" else NC + a) * P
                        last = pe.matmul(mixed[:, :], win_s[:, col:col + P], xnT[:, :], start=True, stop=True)
                    elif what == "bc":
                        for c in range(NC):
                            last = pe.matmul(mixed[0:2 * NS, :], wx_s[:, c, :], u[:, c, :],
                                             start=(c == 0), stop=(c == NC - 1))
                    elif what == "dl":
                        for c in range(NC):
                            last = pe.matmul(mixed[:, :], wdt_s[:, c, a * P:(a + 1) * P], u[:, c, :],
                                             start=(c == 0), stop=(c == NC - 1))
                    elif what == "gy":
                        last = transposes(mixed, y_s)
                    elif what == "proj":
                        for b in range(NB):
                            for c in range(NC):
                                last = pe.matmul(mixed_blocks[:, b, :], sz[:, c, b * P:(b + 1) * P], wout_s[:, c, :],
                                                 start=(c == 0), stop=(c == NC - 1))
                    elif what == "split":
                        last = transposes(mixed, xn2)
                    elif what == "route":
                        for b in range(NB):
                            last = pe.matmul(mixed[:, b * E:(b + 1) * E], x2T[:, b * P:(b + 1) * P], gw_s[:, :],
                                             start=True, stop=True)
                    elif what == "eo":
                        for b in range(NB):
                            for f in range(NF):
                                slot = (NF * a + f) % G_SLOTS
                                last = pe.matmul(eo_bank(a, m)[:, b, :], g[:, slot, b * P:(b + 1) * P],
                                                 w2_s[:, a, f, :], start=(f == 0), stop=(f == NF - 1))
                    last.then_inc(mixed_written, 1)
                elif what == "red":
                    c = a // NS
                    if a % NS == 0:
                        pe.wait_ge(skip_made, NC * (m + 1))
                        wait(pe, y_copied, NC * m + c)
                        for b in range(NB):
                            pe.matmul(y_acc[:, b, :], skip[:, c, b * P:(b + 1) * P], ident[:, :],
                                      is_transpose=True, start=(b == 0), stop=False)
                    pe.wait_ge(hc_made, STEPS * m + a + 1)
                    for b in range(NB):
                        last = pe.matmul(y_acc[:, b, :], hc[:, a % RING, b * P:(b + 1) * P], ident[:, :],
                                         is_transpose=True, start=False, stop=(a % NS == NS - 1 and b == NB - 1))
                    last.then_inc(reduced, 1)
                elif what in ("h1", "h3"):
                    e, f = a // NF, a % NF
                    if a == 0:
                        if first:
                            pe.wait_ge(weights_split, NE)
                        pe.wait_ge(x2_split, m + 1)
                    dst = unit_banks(a, m)[0 if what == "h1" else 1]
                    which, freed, made = {"h1": (0, q_made, h1_made), "h3": (1, h3_copied, h3_made)}[what]
                    wait(pe, freed, UNITS * m + a - (1 if is_last(m) and a > 0 else 0))
                    parts = ((w13_hi, x2_hi), (w13_hi, x2_lo), (w13_lo, x2_hi))
                    for i, (w, xx) in enumerate(parts):
                        last = pe.matmul(dst[:, :], w13_at(w, e, which, f), xx[:, :],
                                         start=(i == 0), stop=(i == len(parts) - 1))
                    last.then_inc(made, 1)

            windows(pe, "pe", task)


INPUTS = ["x", "w_in", "b_in", "w_x", "b_x", "w_dt", "b_dt", "w_out", "b_out", "a_log", "d_skip",
          "gate_w", "gate_b", "w13", "w2", "ident", "below"]


def kernel(**inputs):
    import numpy as np
    import concourse.bacc as bacc
    from concourse.bass_utils import run_bass_kernel_spmd

    a = {k: np.asarray(v) for k, v in inputs.items()}

    def halves(w):
        return w.reshape(NC, P, -1).transpose(1, 0, 2)

    up = np.concatenate([a["L0_ffn_sw1"][None], a["L0_ffn_w1"]])
    lin = np.concatenate([a["L0_ffn_sw3"][None], a["L0_ffn_w3"]])
    down = np.concatenate([a["L0_ffn_sw2"][None], a["L0_ffn_w2"]])
    arrays = {
        "x": a["L0_attn_x"],
        "w_in": a["L0_attn_W_in"],
        "b_in": a["L0_attn_b_in"].reshape(4, P).T,
        "w_x": halves(a["L0_attn_W_xproj"]),
        "b_x": a["L0_attn_b_xproj"][:, None],
        "w_dt": halves(a["L0_attn_W_dt"]),
        "b_dt": a["L0_attn_b_dt"].reshape(NC, P).T,
        "w_out": halves(a["L0_attn_W_out"]),
        "b_out": a["L0_attn_b_out"],
        "a_log": halves(a["L0_attn_A_log"]).reshape(P, NC * NS),
        "d_skip": a["L0_attn_D_param"].reshape(NC, P).T,
        "gate_w": a["L0_ffn_gate_w"].T,
        "gate_b": a["L0_ffn_gate_bias"],
        "w13": np.stack([up, lin], 1).transpose(3, 0, 1, 2).reshape(DM, NE * 2 * FI),
        "w2": down.reshape(NE, DM, NF, P).transpose(3, 0, 2, 1),
        "ident": np.eye(P, dtype=np.float32),
        "below": np.broadcast_to(np.tril(np.ones((E, E), np.float32), -1), (P, E, E)),
    }
    nc = bacc.Bacc("TRN2", target_bir_lowering=False, num_devices=1)
    feeds, aps = {}, []
    for name in INPUTS:
        arr = np.ascontiguousarray(arrays[name])
        feeds[f"in_{name}"] = arr
        aps.append(nc.dram_tensor(f"in_{name}", arr.shape, mybir.dt.from_np(arr.dtype), kind="ExternalInput").ap())
    out = nc.dram_tensor("out_0", (SEQS, T, DM), F32, kind="ExternalOutput").ap()
    build(nc, *aps, out)
    result = run_bass_kernel_spmd(nc, [feeds], core_ids=[0])
    return result.results[0]["out_0"]
```
